# Optimizing a Trainium2 kernel written in Bass

```python
import numpy as np
import jax
import jax.numpy as jnp

def _softmax(x, axis=-1):
    return jax.nn.softmax(x, axis=axis)

def _gelu(x):
    return jax.nn.gelu(x, approximate=True)

def _silu(x):
    return jax.nn.silu(x)

def _sigmoid(x):
    return jax.nn.sigmoid(x)

def _layernorm(x, axis=-1, eps=1e-05):
    m = jnp.mean(x, axis=axis, keepdims=True)
    v = jnp.var(x, axis=axis, keepdims=True)
    return (x - m) / jnp.sqrt(v + eps)

def _scatter_add(tgt, idx, src, axis=0):
    return tgt.at[idx].add(src)

def _segment_sum(src, seg, n):
    return jax.ops.segment_sum(src, seg, n)
kernel_name = 'mk_vit_tower_cls_d1_tok_img1024_r4_d450f7'

def setup_inputs(seed: int=0):
    np.random.seed(seed)
    _w = jnp.asarray

    def _rec_inputs():
        import jax
        import jax.numpy as jnp
        _rk = jax.random.key(seed)
        x = -0.00016672 + 0.999947 * jax.random.normal(jax.random.fold_in(_rk, 1), (128, 3, 224, 224), jnp.float32)
        cls_tok = 0.02 * jax.random.normal(jax.random.fold_in(_rk, 5), (1, 1, 256), jnp.float32)
        return (x, cls_tok)
    x, cls_tok = _rec_inputs()

    def _L0_tok_setup():
        import jax, jax.numpy as jnp
        import numpy as np
        PATCH = 16
        key = jax.random.key(seed)
        k1, k2, k3 = jax.random.split(key, 3)
        B, C, H, Wd = (64, 3, 96, 96)
        patch_dim = C * PATCH * PATCH
        embed_dim = 256
        x = jax.random.normal(k1, (B, C, H, Wd), dtype=jnp.float32)
        W = jax.random.normal(k2, (embed_dim, patch_dim), dtype=jnp.float32) * patch_dim ** (-0.5)
        b = jax.random.normal(k3, (embed_dim,), dtype=jnp.float32) * 0.01
        return {'x': x, 'W': W, 'b': b}
    _L0_tok_all = _L0_tok_setup()
    _L0_tok_in = {k: v for k, v in _L0_tok_all.items() if k in ('W', 'b')}
    del _L0_tok_all

    def _L0_attn_setup():
        import jax, jax.numpy as jnp
        import numpy as np
        B, T, D = (2, 512, 256)
        H = 16
        HD = D // H
        DL = 128
        NR = 64
        EPS = 1.1920929e-07

        def _rms_norm(x, w):
            ms = jnp.mean(jnp.square(x), axis=-1, keepdims=True)
            return x * jax.lax.rsqrt(ms + EPS) * w
        key = jax.random.key(seed)
        ks = jax.random.split(key, 10)
        s = 0.02
        return {'x': jax.random.normal(ks[0], (B, T, D), dtype=jnp.float32), 'W_DQ': jax.random.normal(ks[1], (DL, HD), dtype=jnp.float32) * s, 'W_UQ': jax.random.normal(ks[2], (HD, DL), dtype=jnp.float32) * s, 'W_DKV': jax.random.normal(ks[3], (2 * DL, HD), dtype=jnp.float32) * s, 'W_UKV': jax.random.normal(ks[4], (2 * HD, 2 * DL), dtype=jnp.float32) * s, 'W_QR': jax.random.normal(ks[5], (NR, HD), dtype=jnp.float32) * s, 'W_KR': jax.random.normal(ks[6], (NR, HD), dtype=jnp.float32) * s, 'W_O': jax.random.normal(ks[7], (HD, HD), dtype=jnp.float32) * s, 'q_norm_w': jnp.ones((HD,), dtype=jnp.float32), 'k_norm_w': jnp.ones((HD,), dtype=jnp.float32)}
    _L0_attn_all = _L0_attn_setup()
    _L0_attn_in = {k: v for k, v in _L0_attn_all.items() if k in ('W_DQ', 'W_UQ', 'W_DKV', 'W_UKV', 'W_QR', 'W_KR', 'W_O', 'q_norm_w', 'k_norm_w')}
    del _L0_attn_all

    def _L0_ffn_setup():
        import jax, jax.numpy as jnp
        import numpy as np
        B, S, DIM = (4, 1024, 256)
        BASE_COUPLING = 0.1
        NUM_CYCLES = 3

        def _gelu(x):
            return jax.nn.gelu(x, approximate=False)

        def _coupling_net(h, w1, b1, w2, b2, w3, b3, w4, b4):
            h = _gelu(h @ w1 + b1)
            h = _gelu(h @ w2 + b2)
            h = _gelu(h @ w3 + b3)
            return jax.nn.sigmoid(h @ w4 + b4)

        def _global_net(h, w1, b1, w2, b2, w3, b3):
            h = _gelu(h @ w1 + b1)
            h = _gelu(h @ w2 + b2)
            return jax.nn.sigmoid(h @ w3 + b3)

        def _twist(x):
            o_r, o_i, p_r, p_i = jnp.split(x, 4, axis=-1)
            return jnp.concatenate([p_r, -p_i, -o_r, o_i], axis=-1)
        key = jax.random.key(seed)
        ks = jax.random.split(key, 9)
        d = DIM

        def w(k, fan_in, fan_out):
            return jax.random.normal(k, (fan_in, fan_out), dtype=jnp.float32) / np.sqrt(fan_in).astype(np.float32)
        inp = {'x': jax.random.normal(ks[0], (B, S, d), dtype=jnp.float32)}
        cn_dims = [(d, d), (d, d // 2), (d // 2, d // 4), (d // 4, 1)]
        for i, (a, b) in enumerate(cn_dims):
            inp[f'cn_w{i + 1}'] = w(ks[1 + i], a, b)
            inp[f'cn_b{i + 1}'] = jnp.zeros((b,), dtype=jnp.float32)
        gc_dims = [(d, d // 2), (d // 2, d // 4), (d // 4, 1)]
        for i, (a, b) in enumerate(gc_dims):
            inp[f'gc_w{i + 1}'] = w(ks[5 + i], a, b)
            inp[f'gc_b{i + 1}'] = jnp.zeros((b,), dtype=jnp.float32)
        inp['adaptive_range'] = jnp.full((1,), 0.2, dtype=jnp.float32)
        return inp
    _L0_ffn_all = _L0_ffn_setup()
    _L0_ffn_in = {k: v for k, v in _L0_ffn_all.items() if k in ('cn_w1', 'cn_b1', 'cn_w2', 'cn_b2', 'cn_w3', 'cn_b3', 'cn_w4', 'cn_b4', 'gc_w1', 'gc_b1', 'gc_w2', 'gc_b2', 'gc_w3', 'gc_b3', 'adaptive_range')}
    del _L0_ffn_all
    return {'x': x, 'cls_tok': cls_tok, 'L0_tok_W': _L0_tok_in['W'], 'L0_tok_b': _L0_tok_in['b'], 'L0_attn_W_DQ': _L0_attn_in['W_DQ'], 'L0_attn_W_UQ': _L0_attn_in['W_UQ'], 'L0_attn_W_DKV': _L0_attn_in['W_DKV'], 'L0_attn_W_UKV': _L0_attn_in['W_UKV'], 'L0_attn_W_QR': _L0_attn_in['W_QR'], 'L0_attn_W_KR': _L0_attn_in['W_KR'], 'L0_attn_W_O': _L0_attn_in['W_O'], 'L0_attn_q_norm_w': _L0_attn_in['q_norm_w'], 'L0_attn_k_norm_w': _L0_attn_in['k_norm_w'], 'L0_ffn_cn_w1': _L0_ffn_in['cn_w1'], 'L0_ffn_cn_b1': _L0_ffn_in['cn_b1'], 'L0_ffn_cn_w2': _L0_ffn_in['cn_w2'], 'L0_ffn_cn_b2': _L0_ffn_in['cn_b2'], 'L0_ffn_cn_w3': _L0_ffn_in['cn_w3'], 'L0_ffn_cn_b3': _L0_ffn_in['cn_b3'], 'L0_ffn_cn_w4': _L0_ffn_in['cn_w4'], 'L0_ffn_cn_b4': _L0_ffn_in['cn_b4'], 'L0_ffn_gc_w1': _L0_ffn_in['gc_w1'], 'L0_ffn_gc_b1': _L0_ffn_in['gc_b1'], 'L0_ffn_gc_w2': _L0_ffn_in['gc_w2'], 'L0_ffn_gc_b2': _L0_ffn_in['gc_b2'], 'L0_ffn_gc_w3': _L0_ffn_in['gc_w3'], 'L0_ffn_gc_b3': _L0_ffn_in['gc_b3'], 'L0_ffn_adaptive_range': _L0_ffn_in['adaptive_range']}

def reference(x, cls_tok, L0_tok_W, L0_tok_b, L0_attn_W_DQ, L0_attn_W_UQ, L0_attn_W_DKV, L0_attn_W_UKV, L0_attn_W_QR, L0_attn_W_KR, L0_attn_W_O, L0_attn_q_norm_w, L0_attn_k_norm_w, L0_ffn_cn_w1, L0_ffn_cn_b1, L0_ffn_cn_w2, L0_ffn_cn_b2, L0_ffn_cn_w3, L0_ffn_cn_b3, L0_ffn_cn_w4, L0_ffn_cn_b4, L0_ffn_gc_w1, L0_ffn_gc_b1, L0_ffn_gc_w2, L0_ffn_gc_b2, L0_ffn_gc_w3, L0_ffn_gc_b3, L0_ffn_adaptive_range):
    import jax
    import jax.numpy as jnp

    def _L0_tok_ref(x, W, b):
        import jax, jax.numpy as jnp
        import numpy as np
        PATCH = 16
        B, C, H, Wd = x.shape
        ph = pw = PATCH
        gh, gw = (H // ph, Wd // pw)
        patches = x.reshape(B, C, gh, ph, gw, pw)
        patches = patches.transpose(0, 2, 4, 1, 3, 5).reshape(B, gh * gw, C * ph * pw)
        out = jnp.einsum('bnp,dp->bnd', patches, W) + b
        return out

    def _L0_attn_ref(x, W_DQ, W_UQ, W_DKV, W_UKV, W_QR, W_KR, W_O, q_norm_w, k_norm_w):
        import jax, jax.numpy as jnp
        import numpy as np
        B, T, D = (2, 512, 256)
        H = 16
        HD = D // H
        DL = 128
        NR = 64
        EPS = 1.1920929e-07

        def _rms_norm(x, w):
            ms = jnp.mean(jnp.square(x), axis=-1, keepdims=True)
            return x * jax.lax.rsqrt(ms + EPS) * w
        b, t, d = x.shape
        scale = HD ** (-0.5)
        xh = x.reshape(b, t, H, HD).transpose(0, 2, 1, 3)
        c_q = jnp.einsum('bhtd,ld->bhtl', xh, W_DQ)
        q_c = jnp.einsum('bhtl,dl->bhtd', c_q, W_UQ)
        q_c_norm = _rms_norm(q_c, q_norm_w)
        q_r = jnp.einsum('bhtd,rd->bhtr', q_c_norm, W_QR)
        q = jnp.concatenate([q_c_norm, q_r], axis=-1)
        c_kv = jnp.einsum('bhtd,ld->bhtl', xh, W_DKV)
        kv = jnp.einsum('bhtl,dl->bhtd', c_kv, W_UKV)
        k_c, v_c = (kv[..., :HD], kv[..., HD:])
        k_c_norm = _rms_norm(k_c, k_norm_w)
        k_r = jnp.einsum('bhtd,rd->bhtr', xh, W_KR)
        k = jnp.concatenate([k_c_norm, k_r], axis=-1)
        scores = jnp.einsum('bhqd,bhkd->bhqk', q, k) * scale
        causal = jnp.triu(jnp.full((t, t), -jnp.inf, dtype=scores.dtype), k=1)
        attn = jax.nn.softmax(scores + causal, axis=-1)
        ctx = jnp.einsum('bhqk,bhkd->bhqd', attn, v_c)
        out = jnp.einsum('bhtd,od->bhto', ctx, W_O)
        return out.transpose(0, 2, 1, 3).reshape(b, t, d)

    def _L0_ffn_ref(x, cn_w1, cn_b1, cn_w2, cn_b2, cn_w3, cn_b3, cn_w4, cn_b4, gc_w1, gc_b1, gc_w2, gc_b2, gc_w3, gc_b3, adaptive_range):
        import jax, jax.numpy as jnp
        import numpy as np
        B, S, DIM = (4, 1024, 256)
        BASE_COUPLING = 0.1
        NUM_CYCLES = 3

        def _gelu(x):
            return jax.nn.gelu(x, approximate=False)

        def _coupling_net(h, w1, b1, w2, b2, w3, b3, w4, b4):
            h = _gelu(h @ w1 + b1)
            h = _gelu(h @ w2 + b2)
            h = _gelu(h @ w3 + b3)
            return jax.nn.sigmoid(h @ w4 + b4)

        def _global_net(h, w1, b1, w2, b2, w3, b3):
            h = _gelu(h @ w1 + b1)
            h = _gelu(h @ w2 + b2)
            return jax.nn.sigmoid(h @ w3 + b3)

        def _twist(x):
            o_r, o_i, p_r, p_i = jnp.split(x, 4, axis=-1)
            return jnp.concatenate([p_r, -p_i, -o_r, o_i], axis=-1)
        global_context = x.mean(axis=1, keepdims=True)
        gf = _global_net(global_context, gc_w1, gc_b1, gc_w2, gc_b2, gc_w3, gc_b3)
        out = x
        for _ in range(NUM_CYCLES):
            tf = _coupling_net(out, cn_w1, cn_b1, cn_w2, cn_b2, cn_w3, cn_b3, cn_w4, cn_b4)
            combined = 0.7 * gf + 0.3 * tf
            coupling = BASE_COUPLING + adaptive_range * (combined - 0.5) * 2.0
            out = out + coupling * _twist(out)
        return out
    h = _L0_tok_ref(x, L0_tok_W, L0_tok_b)
    h = jnp.concatenate([jnp.broadcast_to(cls_tok, (h.shape[0], 1, h.shape[2])), h], axis=1)
    h = h + _L0_attn_ref(_layernorm(h, axis=-1), L0_attn_W_DQ, L0_attn_W_UQ, L0_attn_W_DKV, L0_attn_W_UKV, L0_attn_W_QR, L0_attn_W_KR, L0_attn_W_O, L0_attn_q_norm_w, L0_attn_k_norm_w)
    h = h + _L0_ffn_ref(_layernorm(h, axis=-1), L0_ffn_cn_w1, L0_ffn_cn_b1, L0_ffn_cn_w2, L0_ffn_cn_b2, L0_ffn_cn_w3, L0_ffn_cn_b3, L0_ffn_cn_w4, L0_ffn_cn_b4, L0_ffn_gc_w1, L0_ffn_gc_b1, L0_ffn_gc_w2, L0_ffn_gc_b2, L0_ffn_gc_w3, L0_ffn_gc_b3, L0_ffn_adaptive_range)
    return h

_drawn_inputs = setup_inputs


def setup_inputs(seed=0):
    import zlib

    import numpy as np

    out = dict(_drawn_inputs(seed))
    spreads = {'L0_attn_q_norm_w': (1.0, 0.6),
     'L0_attn_k_norm_w': (1.0, 0.6),
     'L0_ffn_cn_b1': (0.0, 2.0),
     'L0_ffn_cn_b2': (0.0, 2.0),
     'L0_ffn_cn_b3': (0.0, 2.0),
     'L0_ffn_gc_b1': (0.0, 0.8),
     'L0_ffn_gc_b2': (0.0, 0.8)}
    factors = {'L0_tok_b': 5.527,
     'L0_attn_W_DQ': 8.0,
     'L0_attn_W_UQ': 8.0,
     'L0_attn_W_DKV': 8.0,
     'L0_attn_W_UKV': 8.0,
     'L0_attn_W_QR': 8.0,
     'L0_attn_W_KR': 8.0,
     'L0_attn_W_O': 8.0,
     'L0_ffn_cn_w1': 7.329,
     'L0_ffn_cn_w2': 7.463,
     'L0_ffn_cn_w3': 5.973,
     'L0_ffn_cn_w4': 7.032,
     'L0_ffn_gc_w1': 8.0,
     'L0_ffn_gc_w2': 8.0,
     'L0_ffn_gc_w3': 5.735}
    for name, (base, spread) in spreads.items():
        noise = np.random.default_rng([zlib.crc32(name.encode()), seed]).standard_normal(out[name].shape)
        drawn = base * np.exp(spread * noise) if base else spread * noise
        out[name] = jnp.asarray(drawn.astype(out[name].dtype))
    for name, factor in factors.items():
        out[name] = (out[name] * factor).astype(out[name].dtype)
    return out
```

```python
from contextlib import ExitStack

import concourse.bass as bass
from concourse import mybir

F32 = mybir.dt.float32
BF16 = mybir.dt.bfloat16
ALU = mybir.AluOpType
ACT = mybir.ActivationFunctionType
AX = mybir.AxisListType

P = 128
D = 256
FT = D // P
H = 16
HD = D // H
SLOT = 32
HG = H // 4
LN_EPS = 1e-5
RMS_EPS = 1.1920929e-07
NEG = -1e30
CYCLES = 3
Q, K, V, R = range(4)


def build(nc, a, out):
    B, _, KT, NP = a["x"].shape
    T = NP + 1
    TS = [P, T - P]
    T1 = TS[1]
    DL = a["wdq"].shape[0]
    NR = a["wqr"].shape[0]
    F1, F2, F3 = a["cn_w1"].shape[1], a["cn_w2"].shape[1], a["cn_w3"].shape[1]
    G1, G2 = a["gc_w1"].shape[1], a["gc_w2"].shape[1]
    N2 = 2 * T

    h1_dram = nc.dram_tensor("h1_scratch", (B, T, D), F32, kind="Internal").ap()

    ctx = ExitStack()
    with ctx:
        def sb(name, shape, dt=F32):
            return ctx.enter_context(nc.sbuf_tensor(name, shape, dt))

        def sem(name):
            return ctx.enter_context(nc.semaphore(name))

        ps = ctx.enter_context(nc.psum_tensor("ps", [P, 8, 512], F32))

        w_tok = sb("w_tok", [P, KT, D])
        tok_add = sb("tok_add", [P, 2, D])
        w_qkv = sb("w_qkv", [P, 4, 8, HD])
        wk_row = sb("wk_row", [P, HD])
        wq_col = sb("wq_col", [P, 1])
        ident = sb("ident", [P, P])
        ident_b = sb("ident_b", [P, P], BF16)
        mask0 = sb("mask0", [P, 4, P], BF16)
        mask1 = sb("mask1", [P, 2, T], BF16)
        power = sb("power", [P, 2 * H])
        wdq = sb("wdq", [DL, HD])
        wuqT = sb("wuqT", [DL, HD])
        wdkv = sb("wdkv", [P, 2, HD])
        wukvT = sb("wukvT", [P, 2, 2 * HD])
        wqr = sb("wqr", [NR, HD])
        wkr = sb("wkr", [NR, HD])
        woT = sb("woT", [HD, HD])
        a_v = sb("a_v", [HD, HD])
        small = sb("small", [HD, 4, HD])

        cn_w1 = sb("cn_w1", [P, FT, F1])
        cn_w2 = sb("cn_w2", [P, F1 // P, F2])
        cn_w3 = sb("cn_w3", [F2, F3])
        cn_w4 = sb("cn_w4", [F3, 1])
        cn_w4r = sb("cn_w4r", [F3, P])
        cn_b1 = sb("cn_b1", [P, F1 // P])
        cn_b2 = sb("cn_b2", [F2, 1])
        cn_b3 = sb("cn_b3", [F3, 1])
        cn_b4 = sb("cn_b4", [P, 2])
        gc_w1 = sb("gc_w1", [P, FT, G1])
        gc_w2 = sb("gc_w2", [G1, G2])
        gc_w3 = sb("gc_w3", [G2, 1])
        gc_w3r = sb("gc_w3r", [G2, P])
        gc_b1 = sb("gc_b1", [G1, 1])
        gc_b2 = sb("gc_b2", [G2, 1])
        gc_b3 = sb("gc_b3", [P, 2])
        ar = sb("ar", [P, 1])
        sign = sb("sign", [P, 1])
        c_tf = sb("c_tf", [P, 1])
        c_gf = sb("c_gf", [P, 1])
        c_base = sb("c_base", [P, 1])

        xb = sb("xb", [P, 2, KT, T])
        h = sb("h", [P, 2, 2, D])
        st = sb("st", [P, 2, 6])
        mv = sb("mv", [P, 2, 2])
        ve = sb("ve", [P, 2, 1])
        rstd = sb("rstd", [P, 2, 1])
        hn = sb("hn", [P, 2, D])
        hnT = sb("hnT", [P, FT, T])
        qkv = sb("qkv", [P, 2, 2, 4, H, SLOT])
        sq = sb("sq", [P, 2, 2, H, HD])
        ss = sb("ss", [P, 2, 2 * H])
        se = sb("se", [P, 2, 2 * H])
        rs = sb("rs", [P, 2, 2 * H])
        qT = sb("qT", [P, 2, HG, T])
        kT = sb("kT", [P, 2, HG, T])
        mx = sb("mx", [P, 2, H, SLOT])
        p0 = sb("p0", [P, 4, HG, T])
        p1 = sb("p1", [P, 4, HG, T1])
        ctxT = sb("ctxT", [P, HG, T])
        rden = sb("rden", [P, 2, H])
        att = sb("att", [P, 2, D])

        hl = sb("hl", [P, 2, 2, 2, D])
        hk = sb("hk", [P, 2, 2, 2, D])
        st2 = sb("st2", [P, 2, 4, 6])
        mv2 = sb("mv2", [P, 2, 4, 2])
        ve2 = sb("ve2", [P, 2, 4])
        rstd2 = sb("rstd2", [P, 2, 4])
        hn2 = sb("hn2", [P, 2, 4, D])
        X = sb("X", [P, 2, FT, N2])
        gsum = sb("gsum", [P, 2, FT, 2])
        ga1 = sb("ga1", [G1, 2, 2])
        ga2 = sb("ga2", [G2, 2, 2])
        gth = sb("gth", [P, 2, 2])
        alpha = sb("alpha", [P, 2, 2])
        a1 = sb("a1", [P, 2, F1 // P, N2])
        a2 = sb("a2", [F2, 2, N2])
        a3 = sb("a3", [F3, 2, N2])
        th = sb("th", [P, 2, N2])
        cs = sb("cs", [P, 2, N2])
        u0 = sb("u0", [P, 2, N2])
        u1 = sb("u1", [P, 2, N2])

        SA, SB, TT, TK, W = 0, (1, 2), (3, 4), 5, (6, 7)

        s_w = sem("weights_loaded")
        s_blk = sem("qkv_blocks_loaded")
        s_cp = sem("pool_constants")
        s_cv = sem("dve_constants")
        s_pw = sem("weight_products_ready")
        s_pwc = sem("weight_products_copied")
        x_loaded = [sem("x_loaded0"), sem("x_loaded1")]
        h1_stored = [sem("h1_stored0"), sem("h1_stored1")]
        tok_done = sem("tok_done")
        h_ready = sem("h_ready")
        bn_done = sem("bn_done")
        mv_ready = sem("mv_ready")
        ve_done = sem("ve_done")
        rstd_done = sem("rstd_done")
        hn_ready = sem("hn_ready")
        hnT_done = sem("hnT_transposed")
        hnT_ready = sem("hnT_ready")
        qkv_done = sem("qkv_done")
        qkv_ready = sem("qkv_ready")
        sq_ready = sem("sq_ready")
        ss_ready = sem("ss_ready")
        se_done = sem("se_done")
        rs_ready = sem("rs_ready")
        qk_normed = sem("qk_normed")
        kw_done = sem("kw_done")
        k_ready = sem("k_ready")
        qk_transposed = sem("qk_transposed")
        qT_ready = sem("qT_ready")
        kT_ready = sem("kT_ready")
        s_done = sem("scores_done")
        s_max = sem("scores_max")
        mx_transposed = sem("mx_transposed")
        mx_added = sem("mx_added")
        t_done = sem("scoresT_done")
        e_done = sem("exp_done")
        m_done = sem("masked")
        pv_done = sem("pv_done")
        ctx0_ready = sem("ctx0_ready")
        ctx1_ready = sem("ctx1_ready")
        ctx_transposed = sem("ctx_transposed")
        rden_done = sem("rden_done")
        att_ready = sem("att_ready")
        h1_ready = sem("h1_ready")

        pool_waits = sem("pool_waits")
        dve_waits = sem("dve_waits")

        def two(name):
            return [sem(f"{name}_c{c}") for c in range(2)]

        hl_loaded, hk_loaded, out_stored = two("hl_loaded"), two("hk_loaded"), two("out_stored")
        bn2_done, mv2_ready, ve2_done, rstd2_done, hn2_ready = (
            two("bn2"), two("mv2"), two("ve2"), two("rstd2"), two("hn2"))
        x_done, x_ready, gsum_ready = two("x_transposed"), two("x_ready"), two("gsum_ready")
        g_done, g_ready, alpha_ready = two("g_done"), two("g_ready"), two("alpha_ready")
        l_done, l_ready = two("layer_done"), two("layer_ready")
        cs_ready, u_ready = two("cs_ready"), two("u_ready")
        u1_ready, xd_ready, xp_ready = two("u1_ready"), two("x_dve"), two("x_pool")
        y_done, y_ready = two("y_transposed"), two("y_ready")

        block = ctx.enter_context(nc.Block())

        small_w = [
            (w_tok[:], a["w_tok"]),
            (tok_add[:, 0, :], a["tok_b"].partition_broadcast(P)),
            (tok_add[:, 1, :], a["tok_b"].partition_broadcast(P)),
            (wk_row[:], a["wk"].partition_broadcast(P)),
            (wdq[:], a["wdq"]), (wuqT[:], a["wuqT"]), (wdkv[:], a["wdkv"]), (wukvT[:], a["wukvT"]),
            (wqr[:], a["wqr"]), (wkr[:], a["wkr"]), (woT[:], a["woT"]),
            (cn_w1[:], a["cn_w1"].rearrange("(t p) m -> p t m", p=P)),
            (cn_w2[:], a["cn_w2"].rearrange("(t p) m -> p t m", p=P)),
            (cn_w3[:], a["cn_w3"]), (cn_w4[:], a["cn_w4"]),
            (cn_b1[:], a["cn_b1"]),
            (cn_b2[:], a["cn_b2"].rearrange("(p o) -> p o", o=1)),
            (cn_b3[:], a["cn_b3"].rearrange("(p o) -> p o", o=1)),
            (cn_b4[:, 0:1], a["cn_b4"].partition_broadcast(P)),
            (gc_w1[:], a["gc_w1"].rearrange("(t p) m -> p t m", p=P)),
            (gc_w2[:], a["gc_w2"]), (gc_w3[:], a["gc_w3"]),
            (gc_b1[:], a["gc_b1"].rearrange("(p o) -> p o", o=1)),
            (gc_b2[:], a["gc_b2"].rearrange("(p o) -> p o", o=1)),
            (gc_b3[:, 0:1], a["gc_b3"].partition_broadcast(P)),
            (ar[:], a["ar"].partition_broadcast(P)),
        ]
        small_q = [(wq_col[SLOT * i:SLOT * i + HD, :], a["wq"].rearrange("(p o) -> p o", o=1))
                   for i in range(4)]
        N_W = 16 * (len(small_w) + len(small_q) + 1)

        def images(eng, both, first, last):
            first()
            both(1, 1)
            with eng.Fori(0, B // 2 - 1) as i:
                both(i * 2 + 2, 0)
                both(i * 2 + 3, 1)
            last(B - 1, 1)

        def later(m, n):
            return not isinstance(m, int) or m >= n

        @block.sync
        def _(sp):
            for dst, src in small_w:
                sp.dma_start(dst, src).then_inc(s_w, 16)
            sp.wait_ge(s_cv, 2)
            for dst, src in small_q:
                sp.dma_start(dst, src).then_inc(s_w, 16)
            sp.wait_ge(s_w, N_W - 16)
            sp.dma_start(tok_add[0:1, 0, :], a["cls"]).then_inc(s_w, 16)

            def load_x(m, par):
                sp.dma_start(xb[:, par, :, 1:T], a["x"][m]).then_inc(x_loaded[par], 16)

            def store_h1(m, par):
                sp.wait_ge(h1_ready, m * 2 + 1)
                sp.dma_start(h1_dram[m, 0:P, :], h[:, par, 0, :]).then_inc(h1_stored[par], 16)
                sp.wait_ge(h1_ready, m * 2 + 2)
                sp.dma_start(h1_dram[m, P:T, :], h[0:T1, par, 1, :]).then_inc(h1_stored[par], 16)

            load_x(0, 0)
            load_x(1, 1)
            sp.wait_ge(s_pwc, 5)
            for n in range(8):
                sp.dma_start(w_qkv[HD * n:HD * n + HD, :, n, :], small[:, :, :]).then_inc(s_blk, 16)
            with sp.Fori(0, B // 2 - 1) as i:
                for par in range(2):
                    sp.wait_ge(tok_done, i * 4 + 2 * par + 2)
                    load_x(i * 2 + 2 + par, par)
                    store_h1(i * 2 + par, par)
            store_h1(B - 2, 0)
            store_h1(B - 1, 1)
            for par in range(2):
                sp.wait_ge(h1_stored[par], 16 * B)

            def load2(dst, i, c, s):
                for t in range(2):
                    src = h1_dram[:, t * P:t * P + TS[t], :].rearrange("(g n) p d -> g p n d", n=2)
                    sp.dma_start(dst[0:TS[t], c, t, :, :], src[i * 2 + c]).then_inc(s[c], 16)

            for c in range(2):
                load2(hl, 0, c, hl_loaded)
                load2(hk, 0, c, hk_loaded)

            def store_out(i, c):
                for t in range(2):
                    sp.wait_ge(y_ready[c], i * 2 + t + 1)
                    dst = out[:, t * P:t * P + TS[t], :].rearrange("(g n) p d -> g p n d", n=2)
                    sp.dma_start(dst[i * 2 + c], hk[0:TS[t], c, t, :, :]).then_inc(out_stored[c], 16)

            if B > 4:
                with sp.Fori(0, B // 4 - 1) as i:
                    for c in range(2):
                        sp.wait_ge(hn2_ready[c], i * 4 + 4)
                        load2(hl, i + 1, c, hl_loaded)
                    for c in range(2):
                        store_out(i, c)
                        sp.wait_ge(out_stored[c], i * 32 + 32)
                        load2(hk, i + 1, c, hk_loaded)
            for c in range(2):
                store_out(B // 4 - 1, c)
            for c in range(2):
                sp.wait_ge(out_stored[c], 32 * (B // 4))

        @block.gpsimd
        def _(pool):
            g = nc.gpsimd
            g.memset(ident[:], 0.0).then_inc(s_cp, 1)
            g.memset(mask0[:], 0.0).then_inc(s_cp, 1)
            g.memset(mask1[:], 0.0).then_inc(s_cp, 1)
            g.memset(sign[:], 1.0).then_inc(s_cp, 1)
            g.memset(power[:], -0.5).then_inc(s_cp, 1)
            pool.wait_ge(s_cp, 5)
            g.affine_select(out=ident[:], in_=ident[:], compare_op=ALU.not_equal, fill=1.0, base=0,
                            pattern=[[-1, P]], channel_multiplier=1).then_inc(s_cp, 1)
            g.affine_select(out=mask0[:], in_=mask0[:], compare_op=ALU.is_ge, fill=NEG, base=0,
                            pattern=[[0, 4], [-1, P]], channel_multiplier=1).then_inc(s_cp, 1)
            g.affine_select(out=mask1[:], in_=mask1[:], compare_op=ALU.is_ge, fill=NEG, base=P,
                            pattern=[[0, 2], [-1, T]], channel_multiplier=1).then_inc(s_cp, 1)
            g.affine_select(out=sign[:], in_=sign[:], compare_op=ALU.is_ge, fill=-1.0, base=P // 2 - 1,
                            pattern=[[0, 1]], channel_multiplier=-1).then_inc(s_cp, 1)

            def wait(semaphore, value):
                pool.wait_ge(semaphore, value).then_inc(pool_waits, 1)

            def norm(m, t):
                M = TS[t]
                n = m * 2 + t + 1
                wait(mv_ready, n)
                g.tensor_scalar(ve[:M, t, :], mv[:M, t, 1:2], LN_EPS, None, ALU.add).then_inc(ve_done, 1)
                pool.wait_ge(ve_done, n)
                g.tensor_tensor(rstd[:M, t, :], ve[:M, t, :], power[:M, 0:1], ALU.pow).then_inc(rstd_done, 1)

            def norm_apply(m, par, t):
                M = TS[t]
                wait(rstd_done, m * 2 + t + 1)
                g.tensor_scalar(hn[:M, t, :], h[:M, par, t, :], mv[:M, t, 0:1], rstd[:M, t, :],
                                ALU.subtract, ALU.mult).then_inc(hn_ready, 1)

            def squares(m, par, t):
                M = TS[t]
                pool.wait_ge(qkv_ready, m * 4 + 2 * t + 2)
                if later(m, 1):
                    pool.wait_ge(ss_ready, m * 2 - 1 + t)
                g.tensor_tensor(sq[:M, t], qkv[:M, par, t, Q:K + 1, :, 0:HD], qkv[:M, par, t, Q:K + 1, :, 0:HD],
                                ALU.mult).then_inc(sq_ready, 1)

            def rms(m, t):
                M = TS[t]
                n = m * 2 + t + 1
                wait(ss_ready, n)
                g.tensor_scalar(se[:M, t, :], ss[:M, t, :], 1.0 / HD, RMS_EPS, ALU.mult, ALU.add)\
                 .then_inc(se_done, 1)
                pool.wait_ge(se_done, n)
                g.tensor_tensor(rs[:M, t, :], se[:M, t, :], power[:M, :], ALU.pow).then_inc(rs_ready, 1)

            def k_sum(m, par, t):
                M = TS[t]
                n = m * 2 + t + 1
                pool.wait_ge(qk_normed, n)
                k = qkv[:M, par, t, K, :, 0:HD]
                wk = wk_row[:M, :].rearrange("p (o d) -> p o d", o=1).to_broadcast([M, H, HD])
                g.tensor_tensor(k, k, wk, ALU.mult).then_inc(kw_done, 1)
                pool.wait_ge(kw_done, n)
                g.tensor_tensor(k, k, qkv[:M, par, t, R, :, 0:HD], ALU.add).then_inc(k_ready, 1)

            def select(m, i):
                wait(e_done, m * 12 + 3 * i + 2)
                v = p0[:, i, :, 0:P]
                g.affine_select(out=v, in_=v, compare_op=ALU.is_ge, fill=0.0, base=0,
                                pattern=[[0, HG], [1, P]], channel_multiplier=-1).then_inc(m_done, 1)
                wait(e_done, m * 12 + 3 * i + 3)
                v = p1[:T1, i, :, :]
                g.affine_select(out=v, in_=v, compare_op=ALU.is_ge, fill=0.0, base=0,
                                pattern=[[0, HG], [1, T1]], channel_multiplier=-1).then_inc(m_done, 1)

            def residual(m, par):
                for t in range(2):
                    M = TS[t]
                    pool.wait_ge(att_ready, m * 2 + t + 1)
                    g.tensor_tensor(h[:M, par, t, :], h[:M, par, t, :], att[:M, t, :], ALU.add)\
                     .then_inc(h1_ready, 1)

            def stage(m, par, both=True):
                for t in range(2):
                    norm(m, t)
                for t in range(2):
                    norm_apply(m, par, t)
                if both:
                    select(m - 1, 0)
                    select(m - 1, 1)
                squares(m, par, 0)
                rms(m, 0)
                squares(m, par, 1)
                k_sum(m, par, 0)
                rms(m, 1)
                if both:
                    select(m - 1, 2)
                k_sum(m, par, 1)
                if both:
                    select(m - 1, 3)
                    residual(m - 1, 1 - par)

            def last(m, par):
                for i in range(4):
                    select(m, i)
                residual(m, par)

            pool.wait_ge(s_w, N_W)
            images(pool, stage, lambda: stage(0, 0, False), last)

            def norm2(i, c):
                for t in range(2):
                    M = TS[t]
                    wait(mv2_ready[c], i * 4 + 2 * t + 2)
                    g.tensor_scalar(ve2[:M, c, 2 * t:2 * t + 2], mv2[:M, c, 2 * t:2 * t + 2, 1], LN_EPS, None,
                                    ALU.add).then_inc(ve2_done[c], 1)
                    pool.wait_ge(ve2_done[c], i * 2 + t + 1)
                    g.tensor_tensor(rstd2[:M, c, 2 * t:2 * t + 2], ve2[:M, c, 2 * t:2 * t + 2],
                                    power[:M, 0:2], ALU.pow).then_inc(rstd2_done[c], 1)
                    wait(rstd2_done[c], i * 2 + t + 1)
                    for n in range(2):
                        k = 2 * t + n
                        g.tensor_scalar(hn2[:M, c, k, :], hl[:M, c, t, n, :], mv2[:M, c, k, 0:1],
                                        rstd2[:M, c, k:k + 1], ALU.subtract, ALU.mult)\
                         .then_inc(hn2_ready[c], 1)

            def update_x1(i, c, cyc):
                n = i * CYCLES + cyc + 1
                pool.wait_ge(cs_ready[c], n)
                pool.wait_ge(u_ready[c], n)
                pool.wait_ge(u1_ready[c], n)
                g.tensor_tensor(X[:, c, 1, :], X[:, c, 1, :], u1[:, c, :], ALU.subtract)\
                 .then_inc(xp_ready[c], 1)

            def pass2(i):
                for c in range(2):
                    norm2(i, c)
                for cyc in range(CYCLES):
                    for c in range(2):
                        update_x1(i, c, cyc)

            with pool.Fori(0, B // 4) as i:
                pass2(i)

        @block.scalar
        def _(act):
            s = nc.scalar

            def copy(o, i_):
                return s.activation(o, i_, ACT.Copy)

            def exps(m, i):
                for jj in range(2):
                    act.wait_ge(t_done, m * 12 + 3 * i + jj + 1)
                    s.activation(p0[:, i, 2 * jj:2 * jj + 2, :],
                                 ps[:, TT[jj], 0:N2].rearrange("p (a b) -> p a b", b=T),
                                 ACT.Exp).then_inc(e_done, 1)
                act.wait_ge(t_done, m * 12 + 3 * i + 3)
                s.activation(p1[:T1, i, :, :], ps[:T1, TK, 0:4 * T1].rearrange("p (a b) -> p a b", b=T1),
                             ACT.Exp).then_inc(e_done, 1)

            def hnT_copy(m):
                act.wait_ge(hnT_done, m + 1)
                copy(hnT[:], ps[:, W[0], 0:N2].rearrange("p (f n) -> p f n", f=FT)).then_inc(hnT_ready, 1)

            def qkv_copy(m, par, t):
                M = TS[t]
                for f in range(FT):
                    act.wait_ge(qkv_done, m * 4 + 2 * t + f + 1)
                    copy(qkv[:M, par, t, :, 8 * f:8 * f + 8, 0:HD],
                         ps[:M, W[1 - f], :].rearrange("p (s h d) -> p s h d", s=4, d=HD)).then_inc(qkv_ready, 1)

            def qT_copy(m, par):
                for jj in range(2):
                    act.wait_ge(qk_transposed, m * 4 + jj + 1)
                    s.activation(qT[:, par, 2 * jj:2 * jj + 2, :],
                                 ps[:, W[1 - jj], 0:N2].rearrange("p (a b) -> p a b", b=T),
                                 ACT.Copy, scale=wq_col[:, 0:1]).then_inc(qT_ready, 1)

            def ctx1(m):
                act.wait_ge(pv_done, m * 2 + 2)
                copy(ctxT[:, 2:4, :], ps[:, W[0], 0:N2].rearrange("p (a b) -> p a b", b=T))\
                    .then_inc(ctx1_ready, 1)

            def stage(m, par, both=True):
                if both:
                    exps(m - 1, 0)
                hnT_copy(m)
                if both:
                    exps(m - 1, 1)
                qkv_copy(m, par, 0)
                if both:
                    exps(m - 1, 2)
                qkv_copy(m, par, 1)
                if both:
                    exps(m - 1, 3)
                    ctx1(m - 1)
                qT_copy(m, par)

            def last(m, par):
                for i in range(4):
                    exps(m, i)
                ctx1(m)

            act.wait_ge(s_cv, 11)
            images(act, stage, lambda: stage(0, 0, False), last)

            def x_copy(i, c):
                for f in range(FT):
                    act.wait_ge(x_done[c], i * 2 + f + 1)
                    copy(X[:, c, f, :], ps[:, 4 * c + f, 0:N2]).then_inc(x_ready[c], 1)

            def gnet(i, c):
                act.wait_ge(g_done[c], i * 3 + 1)
                s.activation(ga1[:, c, :], ps[:G1, 4 * c + 3, 0:2], ACT.Gelu, bias=gc_b1[:, 0:1],
                             scale=1.0 / T).then_inc(g_ready[c], 1)
                act.wait_ge(g_done[c], i * 3 + 2)
                s.activation(ga2[:, c, :], ps[:G2, 4 * c + 3, 0:2], ACT.Gelu, bias=gc_b2[:, 0:1])\
                 .then_inc(g_ready[c], 1)
                act.wait_ge(g_done[c], i * 3 + 3)
                s.activation(gth[:, c, :], ps[:, 4 * c + 3, 0:2], ACT.Tanh, bias=gc_b3[:, 1:2], scale=0.5)\
                 .then_inc(g_ready[c], 1)

            def layer(i, c, cyc, l):
                n = (i * CYCLES + cyc) * 5
                if l == 0:
                    for mt in range(2):
                        act.wait_ge(l_done[c], n + mt + 1)
                        s.activation(a1[:, c, mt, :], ps[:, 4 * c + mt, 0:N2], ACT.Gelu,
                                     bias=cn_b1[:, mt:mt + 1]).then_inc(l_ready[c], 1)
                elif l == 1:
                    act.wait_ge(l_done[c], n + 3)
                    s.activation(a2[:, c, :], ps[:, 4 * c + 2, 0:N2], ACT.Gelu, bias=cn_b2[:, 0:1])\
                     .then_inc(l_ready[c], 1)
                elif l == 2:
                    act.wait_ge(l_done[c], n + 4)
                    s.activation(a3[:, c, :], ps[:F3, 4 * c + 3, 0:N2], ACT.Gelu, bias=cn_b3[:, 0:1])\
                     .then_inc(l_ready[c], 1)
                else:
                    act.wait_ge(l_done[c], n + 5)
                    s.activation(th[:, c, :], ps[:, 4 * c + 2, 0:N2], ACT.Tanh, bias=cn_b4[:, 1:2], scale=0.5)\
                     .then_inc(l_ready[c], 1)

            with act.Fori(0, B // 4) as i:
                for c in range(2):
                    x_copy(i, c)
                for c in range(2):
                    gnet(i, c)
                for cyc in range(CYCLES):
                    for l in range(4):
                        for c in range(2):
                            layer(i, c, cyc, l)

        @block.vector
        def _(dve):
            v = nc.vector
            v.memset(w_qkv[:], 0.0).then_inc(s_cv, 1)
            v.memset(wq_col[:], 0.0).then_inc(s_cv, 1)
            v.memset(mx[:], 0.0).then_inc(s_cv, 1)
            v.memset(qkv[:], 0.0).then_inc(s_cv, 1)
            v.memset(xb[:, :, :, 0:1], 0.0).then_inc(s_cv, 1)
            dve.wait_ge(s_cv, 4)
            v.memset(qkv[:, :, :, K:V + 1, :, HD:HD + 1].rearrange("p a t s h o -> p (a t) (s h) o"), 1.0)\
             .then_inc(s_cv, 1)
            dve.wait_ge(s_w, N_W)
            v.tensor_scalar(wq_col[:], wq_col[:], float(HD) ** -0.5, None, ALU.mult).then_inc(s_cv, 1)
            dve.wait_ge(s_cp, 9)
            v.tensor_copy(ident_b[:], ident[:]).then_inc(s_cv, 1)
            v.tensor_copy(cn_w4r[:], cn_w4[:, 0:1].to_broadcast([F3, P]))
            v.tensor_copy(gc_w3r[:], gc_w3[:, 0:1].to_broadcast([G2, P]))
            v.tensor_scalar(cn_b4[:, 1:2], cn_b4[:, 0:1], 0.5, None, ALU.mult)
            v.tensor_scalar(gc_b3[:, 1:2], gc_b3[:, 0:1], 0.5, None, ALU.mult)
            v.tensor_scalar(c_tf[:], sign[:], ar[:, 0:1], 0.3, ALU.mult, ALU.mult).then_inc(s_cv, 1)
            v.tensor_scalar(c_gf[:], sign[:], ar[:, 0:1], 0.7, ALU.mult, ALU.mult).then_inc(s_cv, 1)
            v.tensor_scalar(c_base[:], sign[:], 0.1, None, ALU.mult).then_inc(s_cv, 1)
            dve.wait_ge(s_pw, 4)
            v.tensor_copy(small[:, Q, :], ps[:HD, 0, 0:HD]).then_inc(s_pwc, 1)
            v.tensor_copy(small[:, K, :], ps[:HD, 1, 0:HD]).then_inc(s_pwc, 1)
            v.tensor_copy(a_v[:], ps[:HD, 2, 0:HD]).then_inc(s_pwc, 1)
            v.tensor_copy(small[:, R, :], ps[:HD, 3, 0:HD]).then_inc(s_pwc, 1)
            dve.wait_ge(s_pw, 5)
            v.tensor_copy(small[:, V, :], ps[:HD, 4, 0:HD]).then_inc(s_pwc, 1)

            def embed(m, par, t):
                M = TS[t]
                dve.wait_ge(tok_done, m * 2 + t + 1)
                v.tensor_tensor(h[:M, par, t, :], ps[:M, W[t], 0:D], tok_add[:M, t, :], ALU.add)\
                 .then_inc(h_ready, 1)

            def stats(m, par, t):
                M = TS[t]
                n = m * 2 + t + 1
                dve.wait_ge(h_ready, n)
                v.bn_stats(st[:M, t, :], h[:M, par, t, :]).then_inc(bn_done, 1)
                dve.wait_ge(bn_done, n).then_inc(dve_waits, 1)
                v.bn_aggr(mv[:M, t, :], st[:M, t, :]).then_inc(mv_ready, 1)

            def add_max(m, par):
                for jj in range(2):
                    dve.wait_ge(mx_transposed, m * 2 + jj + 1)
                    q = qT[:, par, 2 * jj:2 * jj + 2, :]
                    v.tensor_tensor(q, q, ps[:, W[1 - jj], 0:N2].rearrange("p (a b) -> p a b", b=T), ALU.add)\
                     .then_inc(mx_added, 1)

            def rms_sum(m, t):
                M = TS[t]
                dve.wait_ge(sq_ready, m * 2 + t + 1)
                v.tensor_reduce(ss[:M, t, :], sq[:M, t].rearrange("p s h d -> p (s h) d"), AX.X, ALU.add)\
                 .then_inc(ss_ready, 1)

            def rms_mul(m, par, t):
                M = TS[t]
                dve.wait_ge(rs_ready, m * 2 + t + 1)
                qk = qkv[:M, par, t, Q:K + 1, :, 0:HD]
                r = rs[:M, t, :].rearrange("p (s h o) -> p s h o", s=2, o=1).to_broadcast([M, 2, H, HD])
                v.tensor_tensor(qk, qk, r, ALU.mult).then_inc(qk_normed, 1)

            def ctx0(m):
                dve.wait_ge(pv_done, m * 2 + 1)
                v.tensor_copy(ctxT[:, 0:2, :], ps[:, W[1], 0:N2].rearrange("p (a b) -> p a b", b=T))\
                 .then_inc(ctx0_ready, 1)

            def kT_copy(m, par):
                for jj in range(2):
                    dve.wait_ge(qk_transposed, m * 4 + 3 + jj)
                    v.tensor_copy(kT[:, par, 2 * jj:2 * jj + 2, :],
                                  ps[:, W[1 - jj], 0:N2].rearrange("p (a b) -> p a b", b=T)).then_inc(kT_ready, 1)

            def attend(m):
                for t in range(2):
                    M = TS[t]
                    c = ps[:M, W[1 - t], :].rearrange("p (h d) -> p h d", d=SLOT)
                    dve.wait_ge(ctx_transposed, m * 2 + t + 1)
                    v.reciprocal(rden[:M, t, :], c[:, :, HD]).then_inc(rden_done, 1)
                    dve.wait_ge(rden_done, m * 2 + t + 1)
                    if later(m, 1):
                        dve.wait_ge(h1_ready, m * 2 + t - 1)
                    r = rden[:M, t, :].rearrange("p (h o) -> p h o", o=1).to_broadcast([M, H, HD])
                    v.tensor_tensor(att[:M, t, :].rearrange("p (h d) -> p h d", d=HD), c[:, :, 0:HD], r,
                                    ALU.mult).then_inc(att_ready, 1)

            def maxima(m):
                for i in range(4):
                    n = m * 12 + 3 * i
                    dve.wait_ge(s_done, n + 1)
                    v.tensor_reduce(mx[:, 0, i:H:4, HD], ps[:, SA, :].rearrange("p (a b) -> p a b", b=P),
                                    AX.X, ALU.max, negate=True).then_inc(s_max, 1)
                    for jj in range(2):
                        dve.wait_ge(s_done, n + 2 + jj)
                        v.tensor_reduce(mx[:T1, 1, i + 8 * jj:i + 8 * jj + 5:4, HD],
                                        ps[:T1, SB[jj], 0:N2].rearrange("p (a b) -> p a b", b=T),
                                        AX.X, ALU.max, negate=True).then_inc(s_max, 1)

            def stage(m, par, both=True):
                if later(m, 2):
                    dve.wait_ge(h1_stored[par], m * 16 - 16 * par)
                embed(m, par, 0)
                if both:
                    add_max(m - 1, 1 - par)
                stats(m, par, 0)
                embed(m, par, 1)
                stats(m, par, 1)
                for t in range(2):
                    rms_sum(m, t)
                    rms_mul(m, par, t)
                if both:
                    ctx0(m - 1)
                kT_copy(m, par)
                if both:
                    attend(m - 1)
                maxima(m)

            def last(m, par):
                add_max(m, par)
                ctx0(m)
                attend(m)

            images(dve, stage, lambda: stage(0, 0, False), last)

            def stats2(i, c):
                for t in range(2):
                    M = TS[t]
                    dve.wait_ge(hl_loaded[c], i * 32 + 32)
                    for n in range(2):
                        k = 2 * t + n
                        v.bn_stats(st2[:M, c, k, :], hl[:M, c, t, n, :]).then_inc(bn2_done[c], 1)
                        dve.wait_ge(bn2_done[c], i * 4 + k + 1).then_inc(dve_waits, 1)
                        v.bn_aggr(mv2[:M, c, k, :], st2[:M, c, k, :]).then_inc(mv2_ready[c], 1)

            def gsums(i, c):
                dve.wait_ge(x_ready[c], i * 2 + 2)
                v.tensor_reduce(gsum[:, c, :, :], X[:, c, :, :].rearrange("p f (n t) -> p (f n) t", t=T), AX.X,
                                ALU.add).then_inc(gsum_ready[c], 1)

            def alphas(i, c):
                dve.wait_ge(g_ready[c], i * 3 + 3)
                v.tensor_scalar(alpha[:, c, :], gth[:, c, :], c_gf[:, 0:1], c_base[:, 0:1], ALU.mult, ALU.add)\
                 .then_inc(alpha_ready[c], 1)

            def update(i, c, cyc):
                n = i * CYCLES + cyc + 1
                dve.wait_ge(alpha_ready[c], i + 1)
                dve.wait_ge(l_ready[c], n * 5)
                v.tensor_scalar(cs[:, c, 0:T], th[:, c, 0:T], c_tf[:, 0:1], alpha[:, c, 0:1],
                                ALU.mult, ALU.add)
                v.tensor_scalar(cs[:, c, T:N2], th[:, c, T:N2], c_tf[:, 0:1], alpha[:, c, 1:2],
                                ALU.mult, ALU.add).then_inc(cs_ready[c], 1)
                dve.wait_ge(cs_ready[c], n)
                v.tensor_tensor(u0[:, c, :], X[:, c, 1, :], cs[:, c, :], ALU.mult).then_inc(u_ready[c], 1)
                v.tensor_tensor(u1[:, c, :], X[:, c, 0, :], cs[:, c, :], ALU.mult).then_inc(u1_ready[c], 1)
                dve.wait_ge(u_ready[c], n)
                dve.wait_ge(u1_ready[c], n)
                v.tensor_tensor(X[:, c, 0, :], X[:, c, 0, :], u0[:, c, :], ALU.add).then_inc(xd_ready[c], 1)

            def finish(i, c):
                dve.wait_ge(hk_loaded[c], i * 32 + 32)
                for t in range(2):
                    M = TS[t]
                    dve.wait_ge(y_done[c], i * 2 + t + 1)
                    y = hk[:M, c, t, :, :]
                    v.tensor_tensor(y, y, ps[:M, 4 * c + t, :].rearrange("p (n d) -> p n d", n=2), ALU.add)\
                     .then_inc(y_ready[c], 1)

            with dve.Fori(0, B // 4) as i:
                for c in range(2):
                    stats2(i, c)
                for c in range(2):
                    gsums(i, c)
                for c in range(2):
                    alphas(i, c)
                for cyc in range(CYCLES):
                    for c in range(2):
                        update(i, c, cyc)
                for c in range(2):
                    finish(i, c)

        @block.tensor
        def _(pe):
            t_ = nc.tensor
            pe.wait_ge(s_w, N_W)
            t_.matmul(ps[:HD, 0, 0:HD], wdq[:], wuqT[:], start=True, stop=True).then_inc(s_pw, 1)
            for c in range(2):
                mm = t_.matmul(ps[:HD, 1, 0:HD], wdkv[:, c, :], wukvT[:, c, 0:HD], start=c == 0, stop=c == 1)
            mm.then_inc(s_pw, 1)
            for c in range(2):
                mm = t_.matmul(ps[:HD, 2, 0:HD], wukvT[:, c, HD:2 * HD], wdkv[:, c, :], start=c == 0, stop=c == 1)
            mm.then_inc(s_pw, 1)
            t_.matmul(ps[:HD, 3, 0:HD], wkr[:], wqr[:], start=True, stop=True).then_inc(s_pw, 1)
            pe.wait_ge(s_pwc, 3)
            t_.matmul(ps[:HD, 4, 0:HD], a_v[:], woT[:], start=True, stop=True).then_inc(s_pw, 1)
            pe.wait_ge(s_cv, 11)
            pe.wait_ge(s_pwc, 5)
            pe.wait_ge(s_cp, 9)

            def bank(b, n, width):
                return ps[:, b, 0:n * width].rearrange("p (a b) -> p a b", b=width)

            def tok(m, par, t):
                M = TS[t]
                for k in range(KT):
                    mm = t_.matmul(ps[:M, W[t], 0:D], xb[:, par, k, t * P:t * P + M], w_tok[:, k, :],
                                   start=k == 0, stop=k == KT - 1)
                mm.then_inc(tok_done, 1)

            def mxT(m, jj):
                for j2 in range(2):
                    j = 2 * jj + j2
                    for t in range(2):
                        M = TS[t]
                        mm = t_.transpose(ps[:, W[1 - jj], j2 * T + t * P:j2 * T + t * P + M],
                                          mx[:M, t, 4 * j:4 * j + 4, :].rearrange("p h d -> p (h d)"), ident[:M, :M])
                mm.then_inc(mx_transposed, 1)

            def hn_transpose(m):
                for t in range(2):
                    M = TS[t]
                    pe.wait_ge(hn_ready, m * 2 + t + 1)
                    for f in range(FT):
                        mm = t_.transpose(ps[:, W[0], f * T + t * P:f * T + t * P + M],
                                          hn[:M, t, f * P:f * P + P], ident[:M, :M])
                mm.then_inc(hnT_done, 1)

            def project(m, t):
                M = TS[t]
                for f in range(FT):
                    t_.matmul(ps[:M, W[1 - f], :], hnT[:, f, t * P:t * P + M],
                              w_qkv[:].rearrange("p s h d -> p (s h d)"), start=True, stop=True)\
                      .then_inc(qkv_done, 1)

            def scoresT(m, par, i):
                rows = slice(SLOT * i, SLOT * i + SLOT)
                n = m * 12 + 3 * i
                again = i > 0 or later(m, 1)
                for jj in range(2):
                    if again:
                        pe.wait_ge(e_done, n - 2 + jj)
                    for j2 in range(2):
                        j = 2 * jj + j2
                        mm = t_.matmul(ps[:, TT[jj], j2 * T:j2 * T + T], kT[rows, par, j, 0:P], qT[rows, par, j, :],
                                       start=True, stop=True)
                    mm.then_inc(t_done, 1)
                if again:
                    pe.wait_ge(e_done, n)
                for j in range(4):
                    mm = t_.matmul(ps[:T1, TK, j * T1:j * T1 + T1], kT[rows, par, j, P:T], qT[rows, par, j, P:T],
                                   start=True, stop=True)
                mm.then_inc(t_done, 1)

            def pv(m, par, jj):
                if jj == 0:
                    pe.wait_ge(m_done, m * 8 + 8)
                for j2 in range(2):
                    j = 2 * jj + j2
                    for i in range(4):
                        t_.matmul(ps[SLOT * i:SLOT * i + SLOT, W[1 - jj], j2 * T:j2 * T + T],
                                  qkv[:, par, 0, V, 4 * j + i, :], p0[:, i, j, :], start=True, stop=False,
                                  tile_position=(0, SLOT * i))
                    for i in range(4):
                        mm = t_.matmul(ps[SLOT * i:SLOT * i + SLOT, W[1 - jj], j2 * T + P:j2 * T + T],
                                       qkv[:T1, par, 1, V, 4 * j + i, :], p1[:T1, i, j, :], start=False, stop=True,
                                       tile_position=(0, SLOT * i))
                mm.then_inc(pv_done, 1)

            def qk_transpose(m, par, slot, jj):
                for j2 in range(2):
                    j = 2 * jj + j2
                    for t in range(2):
                        M = TS[t]
                        mm = t_.transpose(ps[:, W[1 - jj], j2 * T + t * P:j2 * T + t * P + M],
                                          qkv[:M, par, t, slot, 4 * j:4 * j + 4, :], ident[:M, :M])
                mm.then_inc(qk_transposed, 1)

            def ctx_transpose(m, t):
                M = TS[t]
                for j in range(4):
                    mm = t_.transpose(ps[:M, W[1 - t], j * P:j * P + P], ctxT[:, j, t * P:t * P + M], ident[:, :])
                mm.then_inc(ctx_transposed, 1)

            def scores(m, par):
                for i in range(4):
                    rows = slice(SLOT * i, SLOT * i + SLOT)
                    G3 = m * 12 + 3 * i
                    if i > 0 or later(m, 1):
                        pe.wait_ge(s_max, G3 - 2)
                    t_.matmul(ps[:, SA, :], ident_b[:], mask0[:].rearrange("p a b -> p (a b)"), start=True, stop=False)
                    for j in range(4):
                        mm = t_.matmul(ps[:, SA, j * P:j * P + P], qT[rows, par, j, 0:P], kT[rows, par, j, 0:P],
                                       start=False, stop=j == 3)
                    mm.then_inc(s_done, 1)
                    for jj in range(2):
                        if i > 0 or later(m, 1):
                            pe.wait_ge(s_max, G3 - 1 + jj)
                        t_.matmul(ps[:T1, SB[jj], 0:N2], ident_b[:T1, :T1],
                                  mask1[:T1].rearrange("p a b -> p (a b)"), start=True, stop=False)
                        for j2 in range(2):
                            mm = t_.matmul(ps[:T1, SB[jj], j2 * T:j2 * T + T], qT[rows, par, 2 * jj + j2, P:T],
                                           kT[rows, par, 2 * jj + j2, :], start=False, stop=j2 == 1)
                        mm.then_inc(s_done, 1)

            def after_pv(m):
                pe.wait_ge(ctx0_ready, m + 1)
                pe.wait_ge(ctx1_ready, m + 1)

            def stage(m, par, both=True):
                o, opar = m - 1, 1 - par
                pe.wait_ge(x_loaded[par], m * 8 + 16 - 8 * par)
                if both and later(m, 2):
                    pe.wait_ge(att_ready, o * 2)
                tok(m, par, 0)
                if both:
                    pe.wait_ge(s_max, o * 12 + 12)
                    mxT(o, 0)
                    pe.wait_ge(h_ready, m * 2 + 1)
                    mxT(o, 1)
                    pe.wait_ge(mx_added, o * 2 + 1)
                tok(m, par, 1)
                if both:
                    pe.wait_ge(mx_added, o * 2 + 2)
                    scoresT(o, opar, 0)
                hn_transpose(m)
                if both:
                    scoresT(o, opar, 1)
                if not both:
                    pe.wait_ge(s_blk, 128)
                pe.wait_ge(h_ready, m * 2 + 2)
                pe.wait_ge(hnT_ready, m + 1)
                project(m, 0)
                if both:
                    scoresT(o, opar, 2)
                pe.wait_ge(qkv_ready, m * 4 + 2)
                project(m, 1)
                if both:
                    scoresT(o, opar, 3)
                    pe.wait_ge(qkv_ready, m * 4 + 4)
                    pv(o, opar, 0)
                    pv(o, opar, 1)
                    after_pv(o)
                pe.wait_ge(qk_normed, m * 2 + 2)
                qk_transpose(m, par, Q, 0)
                qk_transpose(m, par, Q, 1)
                pe.wait_ge(k_ready, m * 2 + 2)
                for jj in range(2):
                    pe.wait_ge(qT_ready, m * 2 + jj + 1)
                    qk_transpose(m, par, K, jj)
                for t in range(2):
                    pe.wait_ge(kT_ready, m * 2 + t + 1)
                    if both:
                        ctx_transpose(o, t)
                scores(m, par)

            def last(m, par):
                pe.wait_ge(att_ready, m * 2)
                pe.wait_ge(s_max, m * 12 + 12)
                mxT(m, 0)
                mxT(m, 1)
                pe.wait_ge(mx_added, m * 2 + 2)
                for i in range(4):
                    scoresT(m, par, i)
                pv(m, par, 0)
                pv(m, par, 1)
                after_pv(m)
                for t in range(2):
                    ctx_transpose(m, t)

            images(pe, stage, lambda: stage(0, 0, False), last)

            def x_transpose(i, c):
                for f in range(FT):
                    for t in range(2):
                        M = TS[t]
                        if f == 0:
                            pe.wait_ge(hn2_ready[c], i * 4 + 2 * t + 2)
                        for n in range(2):
                            mm = t_.transpose(ps[:, 4 * c + f, n * T + t * P:n * T + t * P + M],
                                              hn2[:M, c, 2 * t + n, f * P:f * P + P], ident[:M, :M])
                    mm.then_inc(x_done[c], 1)

            def gnet(i, c):
                b = 4 * c + 3
                pe.wait_ge(gsum_ready[c], i + 1)
                for f in range(FT):
                    mm = t_.matmul(ps[:G1, b, 0:2], gc_w1[:, f, :], gsum[:, c, f, :], start=f == 0, stop=f == FT - 1)
                mm.then_inc(g_done[c], 1)
                pe.wait_ge(g_ready[c], i * 3 + 1)
                t_.matmul(ps[:G2, b, 0:2], gc_w2[:], ga1[:, c, :], start=True, stop=True).then_inc(g_done[c], 1)
                pe.wait_ge(g_ready[c], i * 3 + 2)
                t_.matmul(ps[:, b, 0:2], gc_w3r[:], ga2[:, c, :], start=True, stop=True).then_inc(g_done[c], 1)

            def layer(i, c, cyc, l):
                n = (i * CYCLES + cyc) * 5
                if l == 0:
                    for mt in range(2):
                        if cyc:
                            pe.wait_ge(xd_ready[c], i * CYCLES + cyc)
                            pe.wait_ge(xp_ready[c], i * CYCLES + cyc)
                        else:
                            pe.wait_ge(x_ready[c], i * 2 + 2)
                        for f in range(FT):
                            mm = t_.matmul(ps[:, 4 * c + mt, 0:N2], cn_w1[:, f, mt * P:mt * P + P], X[:, c, f, :],
                                           start=f == 0, stop=f == FT - 1)
                        mm.then_inc(l_done[c], 1)
                elif l == 1:
                    for f in range(2):
                        pe.wait_ge(l_ready[c], n + f + 1)
                        mm = t_.matmul(ps[:, 4 * c + 2, 0:N2], cn_w2[:, f, :], a1[:, c, f, :], start=f == 0, stop=f == 1)
                    mm.then_inc(l_done[c], 1)
                elif l == 2:
                    pe.wait_ge(l_ready[c], n + 3)
                    if cyc == 0:
                        pe.wait_ge(g_ready[c], i * 3 + 3)
                    t_.matmul(ps[:F3, 4 * c + 3, 0:N2], cn_w3[:], a2[:, c, :], start=True, stop=True)\
                      .then_inc(l_done[c], 1)
                else:
                    pe.wait_ge(l_ready[c], n + 4)
                    t_.matmul(ps[:, 4 * c + 2, 0:N2], cn_w4r[:], a3[:, c, :], start=True, stop=True)\
                      .then_inc(l_done[c], 1)

            def y_transpose(i, c):
                pe.wait_ge(xd_ready[c], i * CYCLES + CYCLES)
                pe.wait_ge(xp_ready[c], i * CYCLES + CYCLES)
                for t in range(2):
                    M = TS[t]
                    for n in range(2):
                        for f in range(FT):
                            mm = t_.transpose(ps[:M, 4 * c + t, n * D + f * P:n * D + f * P + P],
                                              X[:, c, f, n * T + t * P:n * T + t * P + M], ident[:, :])
                    mm.then_inc(y_done[c], 1)

            def pass2(i, first):
                for c in range(2):
                    if not first:
                        pe.wait_ge(y_ready[c], i * 2)
                    x_transpose(i, c)
                for c in range(2):
                    gnet(i, c)
                for cyc in range(CYCLES):
                    for l in range(4):
                        for c in range(2):
                            layer(i, c, cyc, l)
                for c in range(2):
                    y_transpose(i, c)

            pe.wait_ge(att_ready, 2 * B)
            pass2(0, True)
            if B > 4:
                with pe.Fori(1, B // 4) as i:
                    pass2(i, False)


def kernel(**inputs):
    import numpy as np
    import concourse.bacc as bacc
    from concourse.bass_utils import run_bass_kernel_spmd

    def lay(name, prefix="L0_"):
        return np.asarray(inputs[prefix + name])

    x = np.asarray(inputs["x"])
    B, C, Hh, Ww = x.shape
    S = 16
    gh, gw = Hh // S, Ww // S
    KT = C * S * S // P
    patches = x.reshape(B, C, gh, S, gw, S).transpose(0, 1, 3, 5, 2, 4).reshape(B, KT, P, gh * gw)
    w = lay("tok_W")
    arrays = {
        "x": patches.transpose(0, 2, 1, 3),
        "cls": np.asarray(inputs["cls_tok"]).reshape(1, D),
        "w_tok": w.T.reshape(KT, P, D).transpose(1, 0, 2),
        "tok_b": lay("tok_b"),
        "wdq": lay("attn_W_DQ"), "wuqT": lay("attn_W_UQ").T,
        "wdkv": lay("attn_W_DKV").reshape(2, P, HD).transpose(1, 0, 2),
        "wukvT": lay("attn_W_UKV").T.reshape(2, P, 2 * HD).transpose(1, 0, 2),
        "wqr": lay("attn_W_QR"), "wkr": lay("attn_W_KR"), "woT": lay("attn_W_O").T,
        "wq": lay("attn_q_norm_w"), "wk": lay("attn_k_norm_w"), "ar": lay("ffn_adaptive_range"),
    }
    for n in ("cn_w1", "cn_b1", "cn_w2", "cn_b2", "cn_w3", "cn_b3", "cn_w4", "cn_b4",
              "gc_w1", "gc_b1", "gc_w2", "gc_b2", "gc_w3", "gc_b3"):
        arrays[n] = lay("ffn_" + n)
    arrays["cn_b1"] = arrays["cn_b1"].reshape(-1, P).T

    nc = bacc.Bacc("TRN2", target_bir_lowering=False, num_devices=1)
    feeds, aps = {}, {}
    for n, arr in arrays.items():
        arr = np.ascontiguousarray(arr)
        feeds[f"in_{n}"] = arr
        aps[n] = nc.dram_tensor(f"in_{n}", arr.shape, mybir.dt.from_np(arr.dtype), kind="ExternalInput").ap()
    shape = (B, gh * gw + 1, D)
    out = nc.dram_tensor("out", shape, F32, kind="ExternalOutput").ap()
    build(nc, aps, out)
    r = run_bass_kernel_spmd(nc, [feeds], core_ids=[0])
    return r.results[0]["out"]
```

```python
from contextlib import ExitStack

import concourse.bass as bass
from concourse import mybir

F32 = mybir.dt.float32
BF16 = mybir.dt.bfloat16
F32R = mybir.dt.float32r
ALU = mybir.AluOpType
ACT = mybir.ActivationFunctionType
AX = mybir.AxisListType

P = 128
D = 256
FT = D // P
H = 16
HD = D // H
SLOT = 32
HG = H // 4
LN_EPS = 1e-5
RMS_EPS = 1.1920929e-07
NEG = -1e30
CYCLES = 3
Q, K, V, R = range(4)


def build(nc, a, out):
    B, _, KT, NP = a["x"].shape
    T = NP + 1
    TS = [P, T - P]
    T1 = TS[1]
    DL = a["wdq"].shape[0]
    NR = a["wqr"].shape[0]
    F1, F2, F3 = a["cn_w1"].shape[1], a["cn_w2"].shape[1], a["cn_w3"].shape[1]
    G1, G2 = a["gc_w1"].shape[1], a["gc_w2"].shape[1]
    N2 = 2 * T

    h1_dram = nc.dram_tensor("h1_scratch", (B, T, D), F32, kind="Internal").ap()

    ctx = ExitStack()
    with ctx:
        def sb(name, shape, dt=F32):
            return ctx.enter_context(nc.sbuf_tensor(name, shape, dt))

        def sem(name):
            return ctx.enter_context(nc.semaphore(name))

        ps = ctx.enter_context(nc.psum_tensor("ps", [P, 8, 512], F32))

        w_tok = sb("w_tok", [P, KT, D])
        tok_add = sb("tok_add", [P, 2, D])
        w_qkv = sb("w_qkv", [P, 4, 8, HD])
        wk_row = sb("wk_row", [P, HD])
        wq_col = sb("wq_col", [P, 1])
        ident = sb("ident", [P, P])
        ident_b = sb("ident_b", [P, P], BF16)
        mask0 = sb("mask0", [P, 4, P], BF16)
        mask1 = sb("mask1", [P, 2, T1 + 1], BF16)
        rms_eps = sb("rms_eps", [P, 1])
        power = sb("power", [P, 2 * H])
        wdq = sb("wdq", [DL, HD])
        wuqT = sb("wuqT", [DL, HD])
        wdkv = sb("wdkv", [P, 2, HD])
        wukvT = sb("wukvT", [P, 2, 2 * HD])
        wqr = sb("wqr", [NR, HD])
        wkr = sb("wkr", [NR, HD])
        woT = sb("woT", [HD, HD])
        a_v = sb("a_v", [HD, HD])
        small = sb("small", [HD, 4, HD])

        cn_w1 = sb("cn_w1", [P, FT, F1])
        cn_w2 = sb("cn_w2", [P, F1 // P, F2])
        cn_w3 = sb("cn_w3", [F2, F3])
        cn_w4 = sb("cn_w4", [F3, 1])
        cn_w4r = sb("cn_w4r", [F3, P])
        cn_b1 = sb("cn_b1", [P, F1 // P])
        cn_b2 = sb("cn_b2", [F2, 1])
        cn_b3 = sb("cn_b3", [F3, 1])
        cn_b4 = sb("cn_b4", [P, 2])
        gc_w1 = sb("gc_w1", [P, FT, G1])
        gc_w2 = sb("gc_w2", [G1, G2])
        gc_w3 = sb("gc_w3", [G2, 1])
        gc_w3r = sb("gc_w3r", [G2, P])
        gc_b1 = sb("gc_b1", [G1, 1])
        gc_b2 = sb("gc_b2", [G2, 1])
        gc_b3 = sb("gc_b3", [P, 2])
        ar = sb("ar", [P, 1])
        sign = sb("sign", [P, 1])
        c_tf = sb("c_tf", [P, 1])
        c_gf = sb("c_gf", [P, 1])
        c_base = sb("c_base", [P, 1])

        xb = sb("xb", [P, 2, KT, T])
        h = sb("h", [P, 2, 2, D])
        h1 = sb("h1", [P, 2, 2, D])
        st = sb("st", [P, 2, 6])
        mv = sb("mv", [P, 2, 2])
        ve = sb("ve", [P, 2, 1])
        rstd = sb("rstd", [P, 2, 1])
        hn = sb("hn", [P, 2, D])
        hnT = sb("hnT", [P, FT, T])
        qkv = sb("qkv", [P, 2, 2, 4, H, SLOT])
        sq = sb("sq", [P, 2, 2, H, HD])
        ss = sb("ss", [P, 2, 2 * H])
        ls = sb("ls", [P, 2, 2 * H])
        rs = sb("rs", [P, 2, 2 * H])
        qT = sb("qT", [P, HG, T])
        kT = sb("kT", [P, HG, T])
        qR = sb("qR", [P, HG, T + 1], F32R)
        kR = sb("kR", [P, HG, T + 1], F32R)
        mx = sb("mx", [P, 2, H, SLOT])
        p0 = sb("p0", [P, 4, HG, T])
        p1 = sb("p1", [P, 4, HG, T1])
        ctxT = sb("ctxT", [P, HG, T])
        rden = sb("rden", [P, 2, H])
        att = sb("att", [P, 2, D])

        hl = sb("hl", [P, 2, 2, 2, D])
        hk = sb("hk", [P, 2, 2, 2, D])
        st2 = sb("st2", [P, 2, 4, 6])
        mv2 = sb("mv2", [P, 2, 4, 2])
        ve2 = sb("ve2", [P, 2, 4])
        rstd2 = sb("rstd2", [P, 2, 4])
        hn2 = sb("hn2", [P, 2, 4, D])
        X = sb("X", [P, 2, FT, N2])
        gsum = sb("gsum", [P, 2, FT, 2])
        ga1 = sb("ga1", [G1, 2, 2])
        ga2 = sb("ga2", [G2, 2, 2])
        gth = sb("gth", [P, 2, 2])
        alpha = sb("alpha", [P, 2, 2])
        a1 = sb("a1", [P, 2, F1 // P, N2])
        a2 = sb("a2", [F2, 2, N2])
        a3 = sb("a3", [F3, 2, N2])
        th = sb("th", [P, 2, N2])
        cs = sb("cs", [P, 2, N2])
        u0 = sb("u0", [P, 2, N2])
        u1 = sb("u1", [P, 2, N2])

        SA, SB, TT, TK, W = 0, (1, 2), (3, 4), 5, (6, 7)
        KB = (TK, W[1])
        WQ = ((W[0], W[1]), (W[1], W[0]))

        s_w = sem("weights_loaded")
        s_blk = sem("qkv_blocks_loaded")
        s_cp = sem("pool_constants")
        s_cv = sem("dve_constants")
        s_pw = sem("weight_products_ready")
        s_pwc = sem("weight_products_copied")
        x_loaded = [sem("x_loaded0"), sem("x_loaded1")]
        h1_stored = [sem("h1_stored0"), sem("h1_stored1")]
        tok_done = sem("tok_done")
        h_ready = sem("h_ready")
        bn_done = sem("bn_done")
        mv_ready = sem("mv_ready")
        ve_done = sem("ve_done")
        rstd_done = sem("rstd_done")
        hn_ready = sem("hn_ready")
        hnT_done = sem("hnT_transposed")
        hnT_ready = sem("hnT_ready")
        qkv_done = sem("qkv_done")
        qkv_ready = sem("qkv_ready")
        sq_ready = sem("sq_ready")
        ss_ready = sem("ss_ready")
        ls_ready = sem("log_ready")
        rs_ready = sem("rs_ready")
        qk_normed = sem("qk_normed")
        kw_done = sem("kw_done")
        k_ready = sem("k_ready")
        qk_transposed = sem("qk_transposed")
        qT_ready = sem("qT_ready")
        kT_ready = sem("kT_ready")
        s_done = sem("scores_done")
        s_max = sem("scores_max")
        mx_transposed = sem("mx_transposed")
        mx_added = sem("mx_added")
        t_done = sem("scoresT_done")
        e_done = sem("exp_done")
        m_done = sem("masked")
        pv_done = sem("pv_done")
        ctx0_ready = sem("ctx0_ready")
        ctx1_ready = sem("ctx1_ready")
        ctx_transposed = sem("ctx_transposed")
        rden_done = sem("rden_done")
        att_ready = sem("att_ready")
        h1_ready = sem("h1_ready")

        pool_waits = sem("pool_waits")
        dve_waits = sem("dve_waits")

        def two(name):
            return [sem(f"{name}_c{c}") for c in range(2)]

        hl_loaded, hk_loaded, out_stored = two("hl_loaded"), two("hk_loaded"), two("out_stored")
        bn2_done, mv2_ready, ve2_done, rstd2_done, hn2_ready = (
            two("bn2"), two("mv2"), two("ve2"), two("rstd2"), two("hn2"))
        x_done, x_ready, gsum_ready = two("x_transposed"), two("x_ready"), two("gsum_ready")
        g_done, g_ready, alpha_ready = two("g_done"), two("g_ready"), two("alpha_ready")
        l_done, l_ready = two("layer_done"), two("layer_ready")
        cs_ready, u_ready = two("cs_ready"), two("u_ready")
        u1_ready, xd_ready, xp_ready = two("u1_ready"), two("x_dve"), two("x_pool")
        y_done, y_ready = two("y_transposed"), two("y_ready")

        block = ctx.enter_context(nc.Block())

        small_w = [
            (w_tok[:], a["w_tok"]),
            (tok_add[:, 0, :], a["tok_b"].partition_broadcast(P)),
            (tok_add[:, 1, :], a["tok_b"].partition_broadcast(P)),
            (wk_row[:], a["wk"].partition_broadcast(P)),
            (wdq[:], a["wdq"]), (wuqT[:], a["wuqT"]), (wdkv[:], a["wdkv"]), (wukvT[:], a["wukvT"]),
            (wqr[:], a["wqr"]), (wkr[:], a["wkr"]), (woT[:], a["woT"]),
            (cn_w1[:], a["cn_w1"].rearrange("(t p) m -> p t m", p=P)),
            (cn_w2[:], a["cn_w2"].rearrange("(t p) m -> p t m", p=P)),
            (cn_w3[:], a["cn_w3"]), (cn_w4[:], a["cn_w4"]),
            (cn_b1[:], a["cn_b1"]),
            (cn_b2[:], a["cn_b2"].rearrange("(p o) -> p o", o=1)),
            (cn_b3[:], a["cn_b3"].rearrange("(p o) -> p o", o=1)),
            (cn_b4[:, 0:1], a["cn_b4"].partition_broadcast(P)),
            (gc_w1[:], a["gc_w1"].rearrange("(t p) m -> p t m", p=P)),
            (gc_w2[:], a["gc_w2"]), (gc_w3[:], a["gc_w3"]),
            (gc_b1[:], a["gc_b1"].rearrange("(p o) -> p o", o=1)),
            (gc_b2[:], a["gc_b2"].rearrange("(p o) -> p o", o=1)),
            (gc_b3[:, 0:1], a["gc_b3"].partition_broadcast(P)),
            (ar[:], a["ar"].partition_broadcast(P)),
        ]
        small_q = [(wq_col[SLOT * i:SLOT * i + HD, :], a["wq"].rearrange("(p o) -> p o", o=1))
                   for i in range(4)]
        N_W = 16 * (len(small_w) + len(small_q) + 1)

        def images(eng, step):
            step(0, 0, True, False)
            step(1, 1, True, True)
            with eng.Fori(0, B // 2 - 1) as i:
                step(i * 2 + 2, 0, True, True)
                step(i * 2 + 3, 1, True, True)
            step(B, 0, False, True)

        def later(m, n):
            return not isinstance(m, int) or m >= n

        @block.sync
        def _(sp):
            for dst, src in small_w:
                sp.dma_start(dst, src).then_inc(s_w, 16)
            sp.wait_ge(s_cv, 2)
            for dst, src in small_q:
                sp.dma_start(dst, src).then_inc(s_w, 16)
            sp.wait_ge(s_w, N_W - 16)
            sp.dma_start(tok_add[0:1, 0, :], a["cls"]).then_inc(s_w, 16)

            def load_x(m, par):
                sp.dma_start(xb[:, par, :, 1:T], a["x"][m]).then_inc(x_loaded[par], 16)

            def store_h1(m, par):
                sp.wait_ge(h1_ready, m * 2 + 1)
                sp.dma_start(h1_dram[m, 0:P, :], h1[:, par, 0, :]).then_inc(h1_stored[par], 16)
                sp.wait_ge(h1_ready, m * 2 + 2)
                sp.dma_start(h1_dram[m, P:T, :], h1[0:T1, par, 1, :]).then_inc(h1_stored[par], 16)

            load_x(0, 0)
            load_x(1, 1)
            sp.wait_ge(s_pwc, 5)
            for n in range(8):
                sp.dma_start(w_qkv[HD * n:HD * n + HD, :, n, :], small[:, :, :]).then_inc(s_blk, 16)
            with sp.Fori(0, B // 2 - 1) as i:
                for par in range(2):
                    sp.wait_ge(tok_done, i * 4 + 2 * par + 2)
                    load_x(i * 2 + 2 + par, par)
                    store_h1(i * 2 + par, par)
            store_h1(B - 2, 0)
            store_h1(B - 1, 1)
            for par in range(2):
                sp.wait_ge(h1_stored[par], 16 * B)

            def load2(dst, i, c, s):
                for t in range(2):
                    src = h1_dram[:, t * P:t * P + TS[t], :].rearrange("(g n) p d -> g p n d", n=2)
                    sp.dma_start(dst[0:TS[t], c, t, :, :], src[i * 2 + c]).then_inc(s[c], 16)

            for c in range(2):
                load2(hl, 0, c, hl_loaded)
                load2(hk, 0, c, hk_loaded)

            def store_out(i, c):
                for t in range(2):
                    sp.wait_ge(y_ready[c], i * 2 + t + 1)
                    dst = out[:, t * P:t * P + TS[t], :].rearrange("(g n) p d -> g p n d", n=2)
                    sp.dma_start(dst[i * 2 + c], hk[0:TS[t], c, t, :, :]).then_inc(out_stored[c], 16)

            if B > 4:
                with sp.Fori(0, B // 4 - 1) as i:
                    for c in range(2):
                        sp.wait_ge(hn2_ready[c], i * 4 + 4)
                        load2(hl, i + 1, c, hl_loaded)
                    for c in range(2):
                        store_out(i, c)
                        sp.wait_ge(out_stored[c], i * 32 + 32)
                        load2(hk, i + 1, c, hk_loaded)
            for c in range(2):
                store_out(B // 4 - 1, c)
            for c in range(2):
                sp.wait_ge(out_stored[c], 32 * (B // 4))

        @block.gpsimd
        def _(pool):
            g = nc.gpsimd
            g.memset(ident[:], 0.0).then_inc(s_cp, 1)
            g.memset(mask0[:], 0.0).then_inc(s_cp, 1)
            g.memset(mask1[:], 0.0).then_inc(s_cp, 1)
            g.memset(sign[:], 1.0).then_inc(s_cp, 1)
            g.memset(power[:], -0.5).then_inc(s_cp, 1)
            g.memset(rms_eps[:], RMS_EPS).then_inc(s_cp, 1)
            pool.wait_ge(s_cp, 6)
            g.affine_select(out=ident[:], in_=ident[:], compare_op=ALU.not_equal, fill=1.0, base=0,
                            pattern=[[-1, P]], channel_multiplier=1).then_inc(s_cp, 1)
            g.affine_select(out=mask0[:], in_=mask0[:], compare_op=ALU.is_ge, fill=NEG, base=0,
                            pattern=[[0, 4], [-1, P]], channel_multiplier=1).then_inc(s_cp, 1)
            g.affine_select(out=mask1[:], in_=mask1[:], compare_op=ALU.is_ge, fill=NEG, base=0,
                            pattern=[[0, 2], [-1, T1 + 1]], channel_multiplier=1).then_inc(s_cp, 1)
            g.affine_select(out=sign[:], in_=sign[:], compare_op=ALU.is_ge, fill=-1.0, base=P // 2 - 1,
                            pattern=[[0, 1]], channel_multiplier=-1).then_inc(s_cp, 1)

            def wait(semaphore, value):
                pool.wait_ge(semaphore, value).then_inc(pool_waits, 1)

            def norm(m, t):
                M = TS[t]
                n = m * 2 + t + 1
                wait(mv_ready, n)
                g.tensor_scalar(ve[:M, t, :], mv[:M, t, 1:2], LN_EPS, None, ALU.add).then_inc(ve_done, 1)
                pool.wait_ge(ve_done, n)
                g.tensor_tensor(rstd[:M, t, :], ve[:M, t, :], power[:M, 0:1], ALU.pow).then_inc(rstd_done, 1)

            def k_sum(m, par, t):
                M = TS[t]
                n = m * 2 + t + 1
                pool.wait_ge(qk_normed, n)
                k = qkv[:M, par, t, K, :, 0:HD]
                wk = wk_row[:M, :].rearrange("p (o d) -> p o d", o=1).to_broadcast([M, H, HD])
                g.tensor_tensor(k, k, wk, ALU.mult).then_inc(kw_done, 1)
                pool.wait_ge(kw_done, n)
                g.tensor_tensor(k, k, qkv[:M, par, t, R, :, 0:HD], ALU.add).then_inc(k_ready, 1)

            def select(m, i):
                wait(e_done, m * 12 + 3 * i + 2)
                v = p0[:, i, :, 0:P]
                g.affine_select(out=v, in_=v, compare_op=ALU.is_ge, fill=0.0, base=0,
                                pattern=[[0, HG], [1, P]], channel_multiplier=-1).then_inc(m_done, 1)
                wait(e_done, m * 12 + 3 * i + 3)
                v = p1[:T1, i, :, :]
                g.affine_select(out=v, in_=v, compare_op=ALU.is_ge, fill=0.0, base=0,
                                pattern=[[0, HG], [1, T1]], channel_multiplier=-1).then_inc(m_done, 1)

            def residual(m, par):
                for t in range(2):
                    M = TS[t]
                    pool.wait_ge(att_ready, m * 2 + t + 1)
                    if later(m, 2):
                        pool.wait_ge(h1_stored[par], m * 16 - 16 * par)
                    g.tensor_tensor(h1[:M, par, t, :], h[:M, par, t, :], att[:M, t, :], ALU.add)\
                     .then_inc(h1_ready, 1)

            def step(n, par, new, old):
                if new:
                    norm(n, 0)
                    norm(n, 1)
                if old:
                    select(n - 1, 0)
                    select(n - 1, 1)
                if new:
                    k_sum(n, par, 0)
                if old:
                    select(n - 1, 2)
                    select(n - 1, 3)
                if new:
                    k_sum(n, par, 1)
                if old:
                    residual(n - 1, 1 - par)

            pool.wait_ge(s_w, N_W)
            images(pool, step)

            def norm2(i, c):
                for t in range(2):
                    M = TS[t]
                    wait(mv2_ready[c], i * 4 + 2 * t + 2)
                    g.tensor_scalar(ve2[:M, c, 2 * t:2 * t + 2], mv2[:M, c, 2 * t:2 * t + 2, 1], LN_EPS, None,
                                    ALU.add).then_inc(ve2_done[c], 1)
                    pool.wait_ge(ve2_done[c], i * 2 + t + 1)
                    g.tensor_tensor(rstd2[:M, c, 2 * t:2 * t + 2], ve2[:M, c, 2 * t:2 * t + 2],
                                    power[:M, 0:2], ALU.pow).then_inc(rstd2_done[c], 1)
                    wait(rstd2_done[c], i * 2 + t + 1)
                    for n in range(2):
                        k = 2 * t + n
                        g.tensor_scalar(hn2[:M, c, k, :], hl[:M, c, t, n, :], mv2[:M, c, k, 0:1],
                                        rstd2[:M, c, k:k + 1], ALU.subtract, ALU.mult)\
                         .then_inc(hn2_ready[c], 1)

            def update_x1(i, c, cyc):
                n = i * CYCLES + cyc + 1
                pool.wait_ge(cs_ready[c], n)
                pool.wait_ge(u_ready[c], n)
                pool.wait_ge(u1_ready[c], n)
                g.tensor_tensor(X[:, c, 1, :], X[:, c, 1, :], u1[:, c, :], ALU.subtract)\
                 .then_inc(xp_ready[c], 1)

            def pass2(i):
                for c in range(2):
                    norm2(i, c)
                for cyc in range(CYCLES):
                    for c in range(2):
                        update_x1(i, c, cyc)

            with pool.Fori(0, B // 4) as i:
                pass2(i)

        @block.scalar
        def _(act):
            s = nc.scalar

            def copy(o, i_):
                return s.activation(o, i_, ACT.Copy)

            def exps(m, i):
                for jj in range(2):
                    act.wait_ge(t_done, m * 12 + 3 * i + jj + 1)
                    s.activation(p0[:, i, 2 * jj:2 * jj + 2, :],
                                 ps[:, TT[jj], 0:N2].rearrange("p (a b) -> p a b", b=T),
                                 ACT.Exp).then_inc(e_done, 1)
                act.wait_ge(t_done, m * 12 + 3 * i + 3)
                s.activation(p1[:T1, i, :, :], ps[:T1, TK, 0:4 * T1].rearrange("p (a b) -> p a b", b=T1),
                             ACT.Exp).then_inc(e_done, 1)

            def hnT_copy(m, t):
                act.wait_ge(hnT_done, m * 2 + t + 1)
                a, b = t * P, t * P + TS[t]
                copy(hnT[:, :, a:b], ps[:, W[1 - t], 0:N2].rearrange("p (f n) -> p f n", f=FT)[:, :, a:b])\
                    .then_inc(hnT_ready, 1)

            def qkv_copy(m, par, t, f):
                M = TS[t]
                bank = ps[:M, WQ[t][f], :].rearrange("p (s h d) -> p s h d", s=4, d=HD)
                act.wait_ge(qkv_done, m * 4 + 2 * t + f + 1)
                s.activation(sq[:M, t, :, 8 * f:8 * f + 8, :], bank[:, Q:K + 1], ACT.Square).then_inc(sq_ready, 1)
                copy(qkv[:M, par, t, :, 8 * f:8 * f + 8, 0:HD], bank).then_inc(qkv_ready, 1)

            def rms(m, t):
                M = TS[t]
                n = m * 2 + t + 1
                act.wait_ge(ss_ready, n)
                s.activation(ls[:M, t, :], ss[:M, t, :], ACT.Ln, bias=rms_eps[:M, 0:1], scale=1.0 / HD)\
                 .then_inc(ls_ready, 1)
                act.wait_ge(ls_ready, n)
                s.activation(rs[:M, t, :], ls[:M, t, :], ACT.Exp, scale=-0.5).then_inc(rs_ready, 1)

            def qT_copy(m):
                for jj in range(2):
                    act.wait_ge(qk_transposed, m * 4 + jj + 1)
                    v = ps[:, TT[jj], 0:N2].rearrange("p (a b) -> p a b", b=T)
                    s.activation(qR[:, 2 * jj:2 * jj + 2, 0:T], v, ACT.Copy, scale=wq_col[:, 0:1])\
                     .then_inc(qT_ready, 1)
                    s.activation(qT[:, 2 * jj:2 * jj + 2, :], v, ACT.Copy, scale=wq_col[:, 0:1])\
                     .then_inc(qT_ready, 1)

            def ctx1(m):
                act.wait_ge(pv_done, m * 2 + 2)
                copy(ctxT[:, 2:4, :], ps[:, W[0], 0:N2].rearrange("p (a b) -> p a b", b=T))\
                    .then_inc(ctx1_ready, 1)

            def step(n, par, new, old):
                if old:
                    qT_copy(n - 1)
                if new:
                    hnT_copy(n, 0)
                    qkv_copy(n, par, 0, 0)
                if old:
                    exps(n - 1, 0)
                if new:
                    qkv_copy(n, par, 0, 1)
                if old:
                    exps(n - 1, 1)
                if new:
                    rms(n, 0)
                    hnT_copy(n, 1)
                    qkv_copy(n, par, 1, 0)
                if old:
                    exps(n - 1, 2)
                if new:
                    qkv_copy(n, par, 1, 1)
                if old:
                    exps(n - 1, 3)
                if new:
                    rms(n, 1)
                if old:
                    ctx1(n - 1)

            act.wait_ge(s_cv, 12)
            act.wait_ge(s_cp, 10)
            images(act, step)

            def x_copy(i, c):
                for f in range(FT):
                    act.wait_ge(x_done[c], i * 2 + f + 1)
                    copy(X[:, c, f, :], ps[:, 4 * c + f, 0:N2]).then_inc(x_ready[c], 1)

            def gnet(i, c):
                act.wait_ge(g_done[c], i * 3 + 1)
                s.activation(ga1[:, c, :], ps[:G1, 4 * c + 3, 0:2], ACT.Gelu, bias=gc_b1[:, 0:1],
                             scale=1.0 / T).then_inc(g_ready[c], 1)
                act.wait_ge(g_done[c], i * 3 + 2)
                s.activation(ga2[:, c, :], ps[:G2, 4 * c + 3, 0:2], ACT.Gelu, bias=gc_b2[:, 0:1])\
                 .then_inc(g_ready[c], 1)
                act.wait_ge(g_done[c], i * 3 + 3)
                s.activation(gth[:, c, :], ps[:, 4 * c + 3, 0:2], ACT.Tanh, bias=gc_b3[:, 1:2], scale=0.5)\
                 .then_inc(g_ready[c], 1)

            def layer(i, c, cyc, l):
                n = (i * CYCLES + cyc) * 5
                if l == 0:
                    for mt in range(2):
                        act.wait_ge(l_done[c], n + mt + 1)
                        s.activation(a1[:, c, mt, :], ps[:, 4 * c + mt, 0:N2], ACT.Gelu,
                                     bias=cn_b1[:, mt:mt + 1]).then_inc(l_ready[c], 1)
                elif l == 1:
                    act.wait_ge(l_done[c], n + 3)
                    s.activation(a2[:, c, :], ps[:, 4 * c + 2, 0:N2], ACT.Gelu, bias=cn_b2[:, 0:1])\
                     .then_inc(l_ready[c], 1)
                elif l == 2:
                    act.wait_ge(l_done[c], n + 4)
                    s.activation(a3[:, c, :], ps[:F3, 4 * c + 3, 0:N2], ACT.Gelu, bias=cn_b3[:, 0:1])\
                     .then_inc(l_ready[c], 1)
                else:
                    act.wait_ge(l_done[c], n + 5)
                    s.activation(th[:, c, :], ps[:, 4 * c + 2, 0:N2], ACT.Tanh, bias=cn_b4[:, 1:2], scale=0.5)\
                     .then_inc(l_ready[c], 1)

            with act.Fori(0, B // 4) as i:
                for c in range(2):
                    x_copy(i, c)
                for c in range(2):
                    gnet(i, c)
                for cyc in range(CYCLES):
                    for l in range(4):
                        for c in range(2):
                            layer(i, c, cyc, l)

        @block.vector
        def _(dve):
            v = nc.vector
            v.memset(w_qkv[:], 0.0).then_inc(s_cv, 1)
            v.memset(wq_col[:], 0.0).then_inc(s_cv, 1)
            v.memset(mx[:], 0.0).then_inc(s_cv, 1)
            v.memset(qkv[:], 0.0).then_inc(s_cv, 1)
            v.memset(xb[:, :, :, 0:1], 0.0).then_inc(s_cv, 1)
            v.memset(kR[:, :, T:T + 1].bitcast(F32), 0.0).then_inc(s_cv, 1)
            dve.wait_ge(s_cv, 4)
            v.memset(qkv[:, :, :, K:V + 1, :, HD:HD + 1].rearrange("p a t s h o -> p (a t) (s h) o"), 1.0)\
             .then_inc(s_cv, 1)
            dve.wait_ge(s_w, N_W)
            v.tensor_scalar(wq_col[:], wq_col[:], float(HD) ** -0.5, None, ALU.mult).then_inc(s_cv, 1)
            dve.wait_ge(s_cp, 10)
            v.tensor_copy(ident_b[:], ident[:]).then_inc(s_cv, 1)
            v.tensor_copy(cn_w4r[:], cn_w4[:, 0:1].to_broadcast([F3, P]))
            v.tensor_copy(gc_w3r[:], gc_w3[:, 0:1].to_broadcast([G2, P]))
            v.tensor_scalar(cn_b4[:, 1:2], cn_b4[:, 0:1], 0.5, None, ALU.mult)
            v.tensor_scalar(gc_b3[:, 1:2], gc_b3[:, 0:1], 0.5, None, ALU.mult)
            v.tensor_scalar(c_tf[:], sign[:], ar[:, 0:1], 0.3, ALU.mult, ALU.mult).then_inc(s_cv, 1)
            v.tensor_scalar(c_gf[:], sign[:], ar[:, 0:1], 0.7, ALU.mult, ALU.mult).then_inc(s_cv, 1)
            v.tensor_scalar(c_base[:], sign[:], 0.1, None, ALU.mult).then_inc(s_cv, 1)
            dve.wait_ge(s_pw, 4)
            v.tensor_copy(small[:, Q, :], ps[:HD, 0, 0:HD]).then_inc(s_pwc, 1)
            v.tensor_copy(small[:, K, :], ps[:HD, 1, 0:HD]).then_inc(s_pwc, 1)
            v.tensor_copy(a_v[:], ps[:HD, 2, 0:HD]).then_inc(s_pwc, 1)
            v.tensor_copy(small[:, R, :], ps[:HD, 3, 0:HD]).then_inc(s_pwc, 1)
            dve.wait_ge(s_pw, 5)
            v.tensor_copy(small[:, V, :], ps[:HD, 4, 0:HD]).then_inc(s_pwc, 1)

            def embed(m, par, t):
                M = TS[t]
                dve.wait_ge(tok_done, m * 2 + t + 1)
                if later(m, 2):
                    dve.wait_ge(h1_ready, m * 2 + t - 3)
                v.tensor_tensor(h[:M, par, t, :], ps[:M, W[0], 0:D], tok_add[:M, t, :], ALU.add)\
                 .then_inc(h_ready, 1)

            def stats(m, par, t):
                M = TS[t]
                n = m * 2 + t + 1
                dve.wait_ge(h_ready, n)
                v.bn_stats(st[:M, t, :], h[:M, par, t, :]).then_inc(bn_done, 1)
                dve.wait_ge(bn_done, n).then_inc(dve_waits, 1)
                v.bn_aggr(mv[:M, t, :], st[:M, t, :]).then_inc(mv_ready, 1)

            def hn_apply(m, par, t):
                M = TS[t]
                dve.wait_ge(rstd_done, m * 2 + t + 1)
                v.tensor_scalar(hn[:M, t, :], h[:M, par, t, :], mv[:M, t, 0:1], rstd[:M, t, :],
                                ALU.subtract, ALU.mult).then_inc(hn_ready, 1)

            def add_max(m):
                for jj in range(2):
                    dve.wait_ge(mx_transposed, m * 2 + jj + 1)
                    q = qT[:, 2 * jj:2 * jj + 2, :]
                    v.tensor_tensor(q, q, ps[:, TT[jj], 0:N2].rearrange("p (a b) -> p a b", b=T), ALU.add)\
                     .then_inc(mx_added, 1)

            def rms_sum(m, t):
                M = TS[t]
                dve.wait_ge(sq_ready, m * 4 + 2 * t + 2)
                v.tensor_reduce(ss[:M, t, :], sq[:M, t].rearrange("p s h d -> p (s h) d"), AX.X, ALU.add)\
                 .then_inc(ss_ready, 1)

            def rms_mul(m, par, t):
                M = TS[t]
                dve.wait_ge(rs_ready, m * 2 + t + 1)
                qk = qkv[:M, par, t, Q:K + 1, :, 0:HD]
                r = rs[:M, t, :].rearrange("p (s h o) -> p s h o", s=2, o=1).to_broadcast([M, 2, H, HD])
                v.tensor_tensor(qk, qk, r, ALU.mult).then_inc(qk_normed, 1)

            def ctx0(m):
                dve.wait_ge(pv_done, m * 2 + 1)
                v.tensor_copy(ctxT[:, 0:2, :], ps[:, W[1], 0:N2].rearrange("p (a b) -> p a b", b=T))\
                 .then_inc(ctx0_ready, 1)

            def kT_copy(m):
                for jj in range(2):
                    dve.wait_ge(qk_transposed, m * 4 + 3 + jj)
                    src = ps[:, KB[jj], 0:N2].rearrange("p (a b) -> p a b", b=T)
                    v.tensor_copy(kR[:, 2 * jj:2 * jj + 2, 0:T], src).then_inc(kT_ready, 1)
                    v.tensor_copy(kT[:, 2 * jj:2 * jj + 2, :], src).then_inc(kT_ready, 1)

            def attend(m):
                for t in range(2):
                    M = TS[t]
                    c = ps[:M, TT[t], :].rearrange("p (h d) -> p h d", d=SLOT)
                    dve.wait_ge(ctx_transposed, m * 2 + t + 1)
                    v.reciprocal(rden[:M, t, :], c[:, :, HD]).then_inc(rden_done, 1)
                    dve.wait_ge(rden_done, m * 2 + t + 1)
                    if later(m, 1):
                        dve.wait_ge(h1_ready, m * 2 + t - 1)
                    r = rden[:M, t, :].rearrange("p (h o) -> p h o", o=1).to_broadcast([M, H, HD])
                    v.tensor_tensor(att[:M, t, :].rearrange("p (h d) -> p h d", d=HD), c[:, :, 0:HD], r,
                                    ALU.mult).then_inc(att_ready, 1)

            def maxima(m, i):
                n = m * 12 + 3 * i
                dve.wait_ge(s_done, n + 1)
                v.tensor_reduce(mx[:, 0, i:H:4, HD], ps[:, SA, :].rearrange("p (a b) -> p a b", b=P),
                                AX.X, ALU.max, negate=True).then_inc(s_max, 1)
                for jj in range(2):
                    dve.wait_ge(s_done, n + 2 + jj)
                    v.tensor_reduce(mx[:T1, 1, i + 8 * jj:i + 8 * jj + 5:4, HD],
                                    ps[:T1, SB[jj], 0:2 * (T + 1)].rearrange("p (a b) -> p a b", b=T + 1),
                                    AX.X, ALU.max, negate=True).then_inc(s_max, 1)

            def step(n, par, new, old):
                if new:
                    embed(n, par, 0)
                    stats(n, par, 0)
                if old:
                    kT_copy(n - 1)
                if new:
                    hn_apply(n, par, 0)
                if old:
                    for i in range(3):
                        maxima(n - 1, i)
                if new:
                    embed(n, par, 1)
                    stats(n, par, 1)
                if old:
                    maxima(n - 1, 3)
                    add_max(n - 1)
                if new:
                    hn_apply(n, par, 1)
                    for t in range(2):
                        rms_sum(n, t)
                        rms_mul(n, par, t)
                if old:
                    ctx0(n - 1)
                    attend(n - 1)

            images(dve, step)

            def stats2(i, c):
                for t in range(2):
                    M = TS[t]
                    dve.wait_ge(hl_loaded[c], i * 32 + 32)
                    for n in range(2):
                        k = 2 * t + n
                        v.bn_stats(st2[:M, c, k, :], hl[:M, c, t, n, :]).then_inc(bn2_done[c], 1)
                        dve.wait_ge(bn2_done[c], i * 4 + k + 1).then_inc(dve_waits, 1)
                        v.bn_aggr(mv2[:M, c, k, :], st2[:M, c, k, :]).then_inc(mv2_ready[c], 1)

            def gsums(i, c):
                dve.wait_ge(x_ready[c], i * 2 + 2)
                v.tensor_reduce(gsum[:, c, :, :], X[:, c, :, :].rearrange("p f (n t) -> p (f n) t", t=T), AX.X,
                                ALU.add).then_inc(gsum_ready[c], 1)

            def alphas(i, c):
                dve.wait_ge(g_ready[c], i * 3 + 3)
                v.tensor_scalar(alpha[:, c, :], gth[:, c, :], c_gf[:, 0:1], c_base[:, 0:1], ALU.mult, ALU.add)\
                 .then_inc(alpha_ready[c], 1)

            def update(i, c, cyc):
                n = i * CYCLES + cyc + 1
                dve.wait_ge(alpha_ready[c], i + 1)
                dve.wait_ge(l_ready[c], n * 5)
                v.tensor_scalar(cs[:, c, 0:T], th[:, c, 0:T], c_tf[:, 0:1], alpha[:, c, 0:1],
                                ALU.mult, ALU.add)
                v.tensor_scalar(cs[:, c, T:N2], th[:, c, T:N2], c_tf[:, 0:1], alpha[:, c, 1:2],
                                ALU.mult, ALU.add).then_inc(cs_ready[c], 1)
                dve.wait_ge(cs_ready[c], n)
                v.tensor_tensor(u0[:, c, :], X[:, c, 1, :], cs[:, c, :], ALU.mult).then_inc(u_ready[c], 1)
                v.tensor_tensor(u1[:, c, :], X[:, c, 0, :], cs[:, c, :], ALU.mult).then_inc(u1_ready[c], 1)
                dve.wait_ge(u_ready[c], n)
                dve.wait_ge(u1_ready[c], n)
                v.tensor_tensor(X[:, c, 0, :], X[:, c, 0, :], u0[:, c, :], ALU.add).then_inc(xd_ready[c], 1)

            def finish(i, c):
                dve.wait_ge(hk_loaded[c], i * 32 + 32)
                for t in range(2):
                    M = TS[t]
                    dve.wait_ge(y_done[c], i * 2 + t + 1)
                    y = hk[:M, c, t, :, :]
                    v.tensor_tensor(y, y, ps[:M, 4 * c + t, :].rearrange("p (n d) -> p n d", n=2), ALU.add)\
                     .then_inc(y_ready[c], 1)

            with dve.Fori(0, B // 4) as i:
                for c in range(2):
                    stats2(i, c)
                for c in range(2):
                    gsums(i, c)
                for c in range(2):
                    alphas(i, c)
                for cyc in range(CYCLES):
                    for c in range(2):
                        update(i, c, cyc)
                for c in range(2):
                    finish(i, c)

        @block.tensor
        def _(pe):
            t_ = nc.tensor
            pe.wait_ge(s_w, N_W)
            t_.matmul(ps[:HD, 0, 0:HD], wdq[:], wuqT[:], start=True, stop=True).then_inc(s_pw, 1)
            for c in range(2):
                mm = t_.matmul(ps[:HD, 1, 0:HD], wdkv[:, c, :], wukvT[:, c, 0:HD], start=c == 0, stop=c == 1)
            mm.then_inc(s_pw, 1)
            for c in range(2):
                mm = t_.matmul(ps[:HD, 2, 0:HD], wukvT[:, c, HD:2 * HD], wdkv[:, c, :], start=c == 0, stop=c == 1)
            mm.then_inc(s_pw, 1)
            t_.matmul(ps[:HD, 3, 0:HD], wkr[:], wqr[:], start=True, stop=True).then_inc(s_pw, 1)
            pe.wait_ge(s_pwc, 3)
            t_.matmul(ps[:HD, 4, 0:HD], a_v[:], woT[:], start=True, stop=True).then_inc(s_pw, 1)
            pe.wait_ge(s_cv, 12)
            pe.wait_ge(s_pwc, 5)
            pe.wait_ge(s_cp, 10)

            def bank(b, n, width):
                return ps[:, b, 0:n * width].rearrange("p (a b) -> p a b", b=width)

            def tok(m, par, t, ks=None):
                M = TS[t]
                for k in range(KT) if ks is None else ks:
                    mm = t_.matmul(ps[:M, W[0], 0:D], xb[:, par, k, t * P:t * P + M], w_tok[:, k, :],
                                   start=k == 0, stop=k == KT - 1)
                if ks is None or KT - 1 in ks:
                    mm.then_inc(tok_done, 1)

            def mxT(m, jj):
                for j2 in range(2):
                    j = 2 * jj + j2
                    for t in range(2):
                        M = TS[t]
                        mm = t_.transpose(ps[:, TT[jj], j2 * T + t * P:j2 * T + t * P + M],
                                          mx[:M, t, 4 * j:4 * j + 4, :].rearrange("p h d -> p (h d)"), ident[:M, :M])
                mm.then_inc(mx_transposed, 1)

            def hn_transpose(m, t):
                M = TS[t]
                pe.wait_ge(hn_ready, m * 2 + t + 1)
                for f in range(FT):
                    mm = t_.transpose(ps[:, W[1 - t], f * T + t * P:f * T + t * P + M],
                                      hn[:M, t, f * P:f * P + P], ident[:M, :M])
                mm.then_inc(hnT_done, 1)

            def project(m, t, f):
                M = TS[t]
                t_.matmul(ps[:M, WQ[t][f], :], hnT[:, f, t * P:t * P + M],
                          w_qkv[:].rearrange("p s h d -> p (s h d)"), start=True, stop=True).then_inc(qkv_done, 1)

            def scoresT(m, i):
                rows = slice(SLOT * i, SLOT * i + SLOT)
                n = m * 12 + 3 * i
                again = i > 0 or later(m, 1)
                for jj in range(2):
                    if again:
                        pe.wait_ge(e_done, n - 2 + jj)
                    for j2 in range(2):
                        j = 2 * jj + j2
                        mm = t_.matmul(ps[:, TT[jj], j2 * T:j2 * T + T], kT[rows, j, 0:P], qT[rows, j, :],
                                       start=True, stop=True)
                    mm.then_inc(t_done, 1)
                if again:
                    pe.wait_ge(e_done, n)
                for j in range(4):
                    mm = t_.matmul(ps[:T1, TK, j * T1:j * T1 + T1], kT[rows, j, P:T], qT[rows, j, P:T],
                                   start=True, stop=True)
                mm.then_inc(t_done, 1)

            def pv(m, par, jj):
                if jj == 0:
                    pe.wait_ge(m_done, m * 8 + 8)
                for j2 in range(2):
                    j = 2 * jj + j2
                    for i in range(4):
                        t_.matmul(ps[SLOT * i:SLOT * i + SLOT, W[1 - jj], j2 * T:j2 * T + T],
                                  qkv[:, par, 0, V, 4 * j + i, :], p0[:, i, j, :], start=True, stop=False,
                                  tile_position=(0, SLOT * i))
                    for i in range(4):
                        mm = t_.matmul(ps[SLOT * i:SLOT * i + SLOT, W[1 - jj], j2 * T + P:j2 * T + T],
                                       qkv[:T1, par, 1, V, 4 * j + i, :], p1[:T1, i, j, :], start=False, stop=True,
                                       tile_position=(0, SLOT * i))
                mm.then_inc(pv_done, 1)

            def qk_transpose(m, par, slot, jj):
                bank = TT[jj] if slot == Q else KB[jj]
                for j2 in range(2):
                    j = 2 * jj + j2
                    for t in range(2):
                        M = TS[t]
                        mm = t_.transpose(ps[:, bank, j2 * T + t * P:j2 * T + t * P + M],
                                          qkv[:M, par, t, slot, 4 * j:4 * j + 4, :], ident[:M, :M])
                mm.then_inc(qk_transposed, 1)

            def ctx_transpose(m, t):
                M = TS[t]
                for j in range(4):
                    mm = t_.transpose(ps[:M, TT[t], j * P:j * P + P], ctxT[:, j, t * P:t * P + M], ident[:, :])
                mm.then_inc(ctx_transposed, 1)

            def scores(m, i):
                rows = slice(SLOT * i, SLOT * i + SLOT)
                n = m * 12 + 3 * i
                again = i > 0 or later(m, 1)
                if again:
                    pe.wait_ge(s_max, n - 2)
                for j in range(4):
                    t_.matmul(ps[:, SA, j * P:j * P + P], qR[rows, j, 0:P], kR[rows, j, 0:P],
                              start=j == 0, stop=False)
                t_.matmul(ps[:, SA, :], ident_b[:], mask0[:].rearrange("p a b -> p (a b)"), start=False, stop=True)\
                  .then_inc(s_done, 1)
                for jj in range(2):
                    if again:
                        pe.wait_ge(s_max, n - 1 + jj)
                    bank = ps[:T1, SB[jj], 0:2 * (T + 1)].rearrange("p (a b) -> p a b", b=T + 1)
                    for j2 in range(2):
                        t_.matmul(bank[:, j2, :], qR[rows, 2 * jj + j2, P:T], kR[rows, 2 * jj + j2, :],
                                  start=j2 == 0, stop=False)
                    t_.matmul(bank[:, :, P:T + 1], ident_b[:T1, :T1], mask1[:T1], start=False, stop=True)\
                      .then_inc(s_done, 1)

            def step(n, par, new, old):
                o, opar = n - 1, 1 - par
                if new:
                    pe.wait_ge(x_loaded[par], n * 8 + 16 - 8 * par)
                    if later(n, 1):
                        pe.wait_ge(qkv_ready, n * 4)
                    tok(n, par, 0)
                if old:
                    if later(o, 1):
                        pe.wait_ge(att_ready, o * 2)
                    pe.wait_ge(qk_normed, o * 2 + 2)
                    qk_transpose(o, opar, Q, 0)
                    qk_transpose(o, opar, Q, 1)
                    pe.wait_ge(k_ready, o * 2 + 2)
                    qk_transpose(o, opar, K, 0)
                    qk_transpose(o, opar, K, 1)
                    pe.wait_ge(qT_ready, o * 4 + 4)
                    pe.wait_ge(kT_ready, o * 4 + 4)
                if new:
                    pe.wait_ge(h_ready, n * 2 + 1)
                for i in range(4):
                    if old:
                        scores(o, i)
                    if new and i < 3:
                        tok(n, par, 1, range(i * KT // 3, (i + 1) * KT // 3))
                if new:
                    hn_transpose(n, 0)
                if old:
                    pe.wait_ge(s_max, o * 12 + 12)
                    mxT(o, 0)
                    mxT(o, 1)
                if new:
                    if not old:
                        pe.wait_ge(s_blk, 128)
                    pe.wait_ge(h_ready, n * 2 + 2)
                    pe.wait_ge(hnT_ready, n * 2 + 1)
                    project(n, 0, 0)
                if old:
                    pe.wait_ge(mx_added, o * 2 + 2)
                    scoresT(o, 0)
                if new:
                    project(n, 0, 1)
                if old:
                    scoresT(o, 1)
                if new:
                    pe.wait_ge(qkv_ready, n * 4 + 1)
                    hn_transpose(n, 1)
                    pe.wait_ge(hnT_ready, n * 2 + 2)
                    pe.wait_ge(qkv_ready, n * 4 + 2)
                    project(n, 1, 0)
                if old:
                    scoresT(o, 2)
                if new:
                    project(n, 1, 1)
                if old:
                    scoresT(o, 3)
                    if new:
                        pe.wait_ge(qkv_ready, n * 4 + 4)
                    pv(o, opar, 0)
                    pv(o, opar, 1)
                    pe.wait_ge(ctx0_ready, o + 1)
                    pe.wait_ge(ctx1_ready, o + 1)
                    ctx_transpose(o, 0)
                    ctx_transpose(o, 1)

            images(pe, step)

            def x_transpose(i, c):
                for f in range(FT):
                    for t in range(2):
                        M = TS[t]
                        if f == 0:
                            pe.wait_ge(hn2_ready[c], i * 4 + 2 * t + 2)
                        for n in range(2):
                            mm = t_.transpose(ps[:, 4 * c + f, n * T + t * P:n * T + t * P + M],
                                              hn2[:M, c, 2 * t + n, f * P:f * P + P], ident[:M, :M])
                    mm.then_inc(x_done[c], 1)

            def gnet(i, c):
                b = 4 * c + 3
                pe.wait_ge(gsum_ready[c], i + 1)
                for f in range(FT):
                    mm = t_.matmul(ps[:G1, b, 0:2], gc_w1[:, f, :], gsum[:, c, f, :], start=f == 0, stop=f == FT - 1)
                mm.then_inc(g_done[c], 1)
                pe.wait_ge(g_ready[c], i * 3 + 1)
                t_.matmul(ps[:G2, b, 0:2], gc_w2[:], ga1[:, c, :], start=True, stop=True).then_inc(g_done[c], 1)
                pe.wait_ge(g_ready[c], i * 3 + 2)
                t_.matmul(ps[:, b, 0:2], gc_w3r[:], ga2[:, c, :], start=True, stop=True).then_inc(g_done[c], 1)

            def layer(i, c, cyc, l):
                n = (i * CYCLES + cyc) * 5
                if l == 0:
                    for mt in range(2):
                        if cyc:
                            pe.wait_ge(xd_ready[c], i * CYCLES + cyc)
                            pe.wait_ge(xp_ready[c], i * CYCLES + cyc)
                        else:
                            pe.wait_ge(x_ready[c], i * 2 + 2)
                        for f in range(FT):
                            mm = t_.matmul(ps[:, 4 * c + mt, 0:N2], cn_w1[:, f, mt * P:mt * P + P], X[:, c, f, :],
                                           start=f == 0, stop=f == FT - 1)
                        mm.then_inc(l_done[c], 1)
                elif l == 1:
                    for f in range(2):
                        pe.wait_ge(l_ready[c], n + f + 1)
                        mm = t_.matmul(ps[:, 4 * c + 2, 0:N2], cn_w2[:, f, :], a1[:, c, f, :], start=f == 0, stop=f == 1)
                    mm.then_inc(l_done[c], 1)
                elif l == 2:
                    pe.wait_ge(l_ready[c], n + 3)
                    if cyc == 0:
                        pe.wait_ge(g_ready[c], i * 3 + 3)
                    t_.matmul(ps[:F3, 4 * c + 3, 0:N2], cn_w3[:], a2[:, c, :], start=True, stop=True)\
                      .then_inc(l_done[c], 1)
                else:
                    pe.wait_ge(l_ready[c], n + 4)
                    t_.matmul(ps[:, 4 * c + 2, 0:N2], cn_w4r[:], a3[:, c, :], start=True, stop=True)\
                      .then_inc(l_done[c], 1)

            def y_transpose(i, c):
                pe.wait_ge(xd_ready[c], i * CYCLES + CYCLES)
                pe.wait_ge(xp_ready[c], i * CYCLES + CYCLES)
                for t in range(2):
                    M = TS[t]
                    for n in range(2):
                        for f in range(FT):
                            mm = t_.transpose(ps[:M, 4 * c + t, n * D + f * P:n * D + f * P + P],
                                              X[:, c, f, n * T + t * P:n * T + t * P + M], ident[:, :])
                    mm.then_inc(y_done[c], 1)

            def pass2(i, first):
                for c in range(2):
                    if not first:
                        pe.wait_ge(y_ready[c], i * 2)
                    x_transpose(i, c)
                for c in range(2):
                    gnet(i, c)
                for cyc in range(CYCLES):
                    for l in range(4):
                        for c in range(2):
                            layer(i, c, cyc, l)
                for c in range(2):
                    y_transpose(i, c)

            pe.wait_ge(att_ready, 2 * B)
            pass2(0, True)
            if B > 4:
                with pe.Fori(1, B // 4) as i:
                    pass2(i, False)


def kernel(**inputs):
    import numpy as np
    import concourse.bacc as bacc
    from concourse.bass_utils import run_bass_kernel_spmd

    def lay(name, prefix="L0_"):
        return np.asarray(inputs[prefix + name])

    x = np.asarray(inputs["x"])
    B, C, Hh, Ww = x.shape
    S = 16
    gh, gw = Hh // S, Ww // S
    KT = C * S * S // P
    patches = x.reshape(B, C, gh, S, gw, S).transpose(0, 1, 3, 5, 2, 4).reshape(B, KT, P, gh * gw)
    w = lay("tok_W")
    arrays = {
        "x": patches.transpose(0, 2, 1, 3),
        "cls": np.asarray(inputs["cls_tok"]).reshape(1, D),
        "w_tok": w.T.reshape(KT, P, D).transpose(1, 0, 2),
        "tok_b": lay("tok_b"),
        "wdq": lay("attn_W_DQ"), "wuqT": lay("attn_W_UQ").T,
        "wdkv": lay("attn_W_DKV").reshape(2, P, HD).transpose(1, 0, 2),
        "wukvT": lay("attn_W_UKV").T.reshape(2, P, 2 * HD).transpose(1, 0, 2),
        "wqr": lay("attn_W_QR"), "wkr": lay("attn_W_KR"), "woT": lay("attn_W_O").T,
        "wq": lay("attn_q_norm_w"), "wk": lay("attn_k_norm_w"), "ar": lay("ffn_adaptive_range"),
    }
    for n in ("cn_w1", "cn_b1", "cn_w2", "cn_b2", "cn_w3", "cn_b3", "cn_w4", "cn_b4",
              "gc_w1", "gc_b1", "gc_w2", "gc_b2", "gc_w3", "gc_b3"):
        arrays[n] = lay("ffn_" + n)
    arrays["cn_b1"] = arrays["cn_b1"].reshape(-1, P).T

    nc = bacc.Bacc("TRN2", target_bir_lowering=False, num_devices=1)
    feeds, aps = {}, {}
    for n, arr in arrays.items():
        arr = np.ascontiguousarray(arr)
        feeds[f"in_{n}"] = arr
        aps[n] = nc.dram_tensor(f"in_{n}", arr.shape, mybir.dt.from_np(arr.dtype), kind="ExternalInput").ap()
    shape = (B, gh * gw + 1, D)
    out = nc.dram_tensor("out", shape, F32, kind="ExternalOutput").ap()
    build(nc, aps, out)
    r = run_bass_kernel_spmd(nc, [feeds], core_ids=[0])
    return r.results[0]["out"]
```

```python
from contextlib import ExitStack

import concourse.bass as bass
from concourse import mybir

F32 = mybir.dt.float32
BF16 = mybir.dt.bfloat16
F32R = mybir.dt.float32r
ALU = mybir.AluOpType
ACT = mybir.ActivationFunctionType
AX = mybir.AxisListType

P = 128
D = 256
FT = D // P
H = 16
HD = D // H
SLOT = 32
HG = H // 4
LN_EPS = 1e-5
RMS_EPS = 1.1920929e-07
NEG = -1e30
CYCLES = 3
LN_EXP_SET = 6
Q, K, V, R = range(4)


def head(i, k):
    half = P // 2
    j, g = 4 * (i // 2) + k, i % 2
    return slice(half * g, half * g + half), j, 2 * j + g


def build(nc, a, out):
    B, _, KT, NP = a["x"].shape
    T = NP + 1
    TS = [P, T - P]
    T1 = TS[1]
    TE = T + T % 2
    E1 = TE - P
    DL = a["wdq"].shape[0]
    NR = a["wqr"].shape[0]
    F1, F2, F3 = a["cn_w1"].shape[1], a["cn_w2"].shape[1], a["cn_w3"].shape[1]
    G1, G2 = a["gc_w1"].shape[1], a["gc_w2"].shape[1]
    N2 = 2 * T

    h1_dram = nc.dram_tensor("h1_scratch", (B, T, D), F32, kind="Internal").ap()

    ctx = ExitStack()
    with ctx:
        def sb(name, shape, dt=F32):
            return ctx.enter_context(nc.sbuf_tensor(name, shape, dt))

        def sem(name):
            return ctx.enter_context(nc.semaphore(name))

        ps = ctx.enter_context(nc.psum_tensor("ps", [P, 8, 512], F32))

        w_tok = sb("w_tok", [P, KT, D])
        tok_add = sb("tok_add", [P, 2, D])
        w_qkv = sb("w_qkv", [P, 4, 8, HD])
        wk_row = sb("wk_row", [P, HD])
        wq_row = sb("wq_row", [P, HD])
        ident = sb("ident", [P, P])
        ident_b = sb("ident_b", [P, P], BF16)
        ident_r = sb("ident_r", [P, P], F32R)
        mask0 = sb("mask0", [P, 4, P], BF16)
        mask1 = sb("mask1", [P, 2, E1], BF16)
        rms_eps = sb("rms_eps", [P, 1])
        power = sb("power", [P, 2 * H])
        wdq = sb("wdq", [DL, HD])
        wuqT = sb("wuqT", [DL, HD])
        wdkv = sb("wdkv", [P, 2, HD])
        wukvT = sb("wukvT", [P, 2, 2 * HD])
        wqr = sb("wqr", [NR, HD])
        wkr = sb("wkr", [NR, HD])
        woT = sb("woT", [HD, HD])
        a_v = sb("a_v", [HD, HD])
        small = sb("small", [HD, 4, HD])

        cn_w1 = sb("cn_w1", [P, FT, F1])
        cn_w2 = sb("cn_w2", [P, F1 // P, F2])
        cn_w3 = sb("cn_w3", [F2, F3])
        cn_w4 = sb("cn_w4", [F3, 1])
        cn_w4r = sb("cn_w4r", [F3, P])
        cn_b1 = sb("cn_b1", [P, F1 // P])
        cn_b2 = sb("cn_b2", [F2, 1])
        cn_b3 = sb("cn_b3", [F3, 1])
        cn_b4 = sb("cn_b4", [P, 2])
        gc_w1 = sb("gc_w1", [P, FT, G1])
        gc_w2 = sb("gc_w2", [G1, G2])
        gc_w3 = sb("gc_w3", [G2, 1])
        gc_w3r = sb("gc_w3r", [G2, P])
        gc_b1 = sb("gc_b1", [G1, 1])
        gc_b2 = sb("gc_b2", [G2, 1])
        gc_b3 = sb("gc_b3", [P, 2])
        ar = sb("ar", [P, 1])
        sign = sb("sign", [P, 1])
        c_tf = sb("c_tf", [P, 1])
        c_gf = sb("c_gf", [P, 1])
        c_base = sb("c_base", [P, 1])

        xb = sb("xb", [P, 2, KT, T])
        h = sb("h", [P, 2, 2, D])
        h1 = sb("h1", [P, 2, 2, D])
        st = sb("st", [P, 2, 6])
        mv = sb("mv", [P, 2, 2])
        ve = sb("ve", [P, 2, 1])
        rstd = sb("rstd", [P, 2, 1])
        hn = sb("hn", [P, 2, D])
        hnT = sb("hnT", [P, FT, T])
        qkv = sb("qkv", [P, 2, 2, 4, H, SLOT])
        sq = sb("sq", [P, 2, 2, H, HD])
        ss = sb("ss", [P, 2, 2 * H])
        ls = sb("ls", [P, 2, 2 * H])
        rs = sb("rs", [P, 2, 2 * H])
        xh = sb("xh", [P, 2, 2 * H])
        y2 = sb("y2", [P, 2, 2 * H])
        rms = sb("rms", [P, 2, 2 * H])
        q2 = sb("q2", [P, 2, H, 4, HD], F32R)
        k2 = sb("k2", [P, 2, H, 4, HD], F32R)
        qT = sb("qT", [P, H // 2, TE], F32R)
        kT = sb("kT", [P, H // 2, TE], F32R)
        mx = sb("mx", [P, 2, H])
        mxT = sb("mxT", [P, TE], F32R)
        p0 = sb("p0", [P, 4, 4, T])
        p1 = sb("p1", [P, 4, 4, T1])
        ctxT = sb("ctxT", [P, HG, T])
        rden = sb("rden", [P, 2, H])
        att = sb("att", [P, 2, D])

        hl = sb("hl", [P, 2, 2, 2, D])
        hk = sb("hk", [P, 2, 2, 2, D])
        st2 = sb("st2", [P, 2, 4, 6])
        mv2 = sb("mv2", [P, 2, 4, 2])
        ve2 = sb("ve2", [P, 2, 4])
        rstd2 = sb("rstd2", [P, 2, 4])
        hn2 = sb("hn2", [P, 2, 4, D])
        X = sb("X", [P, 2, 3, FT, N2])
        gsum = sb("gsum", [P, 2, FT, 2])
        ga1 = sb("ga1", [G1, 2, 2])
        ga2 = sb("ga2", [G2, 2, 2])
        gth = sb("gth", [P, 2, 2])
        alpha = sb("alpha", [P, 2, 2])
        a1 = sb("a1", [P, 2, F1 // P, N2])
        a2 = sb("a2", [F2, 2, N2])
        a3 = sb("a3", [F3, 2, N2])
        th = sb("th", [P, 2, N2])
        base = sb("base", [P, 2, FT, N2])
        u0 = sb("u0", [P, 2, N2])
        u1 = sb("u1", [P, 2, N2])

        SA, SB, TT, TK, W = 0, (1, 2), (3, 4), 5, (6, 7)
        QB = (TK, W[1], TT[0], TT[1])
        KB = (SB[0], SB[1], W[0], TK)
        TOK = (SA, W[0])
        WQ = ((W[0], W[1]), (W[1], W[0]))

        s_w = sem("weights_loaded")
        s_blk = sem("qkv_blocks_loaded")
        s_cp = sem("pool_constants")
        s_cv = sem("dve_constants")
        s_pw = sem("weight_products_ready")
        s_pwc = sem("weight_products_copied")
        x_loaded = [sem("x_loaded0"), sem("x_loaded1")]
        h1_stored = [sem("h1_stored0"), sem("h1_stored1")]
        tok_done = sem("tok_done")
        h_ready = sem("h_ready")
        bn_done = sem("bn_done")
        mv_ready = sem("mv_ready")
        ve_done = sem("ve_done")
        rstd_done = sem("rstd_done")
        hn_ready = sem("hn_ready")
        hnT_done = sem("hnT_transposed")
        hnT_ready = sem("hnT_ready")
        qkv_done = sem("qkv_done")
        qkv_ready = sem("qkv_ready")
        sq_ready = sem("sq_ready")
        ss_ready = sem("ss_ready")
        ls_ready = sem("log_ready")
        rs_ready = sem("rs_ready")
        xh_ready = sem("xh_ready")
        y2_ready = sem("y2_ready")
        y2x_ready = sem("y2x_ready")
        rms_ready = sem("rms_ready")
        qk_normed = sem("qk_normed")
        kw_done = sem("kw_done")
        q_high = sem("q_high_parts")
        k_high = sem("k_high_parts")
        q2_ready = sem("q2_ready")
        k2_ready = sem("k2_ready")
        mxT_ready = sem("mxT_ready")
        k_ready = sem("k_ready")
        qk_transposed = sem("qk_transposed")
        qT_ready = sem("qT_ready")
        kT_ready = sem("kT_ready")
        s_done = sem("scores_done")
        s_max = sem("scores_max")
        mx_transposed = sem("mx_transposed")
        t_done = sem("scoresT_done")
        e_done = sem("exp_done")
        m_done = sem("masked")
        pv_done = sem("pv_done")
        ctx0_ready = sem("ctx0_ready")
        ctx1_ready = sem("ctx1_ready")
        ctx_transposed = sem("ctx_transposed")
        rden_done = sem("rden_done")
        att_ready = sem("att_ready")
        h1_ready = sem("h1_ready")

        pool_waits = sem("pool_waits")
        dve_waits = sem("dve_waits")

        def two(name):
            return [sem(f"{name}_c{c}") for c in range(2)]

        hl_loaded, hk_loaded, out_stored = two("hl_loaded"), two("hk_loaded"), two("out_stored")
        bn2_done, mv2_ready, ve2_done, rstd2_done, hn2_ready = (
            two("bn2"), two("mv2"), two("ve2"), two("rstd2"), two("hn2"))
        x_done, x_ready, gsum_ready = two("x_transposed"), two("x_ready"), two("gsum_ready")
        g_done, g_ready, alpha_ready = two("g_done"), two("g_ready"), two("alpha_ready")
        l_done, l_ready = two("layer_done"), two("layer_ready")
        base_ready, u0_ready, u1_ready = two("base_ready"), two("u0_ready"), two("u1_ready")
        x0_new, x1_new = two("x0_new"), two("x1_new")
        y_done, y_ready = two("y_transposed"), two("y_ready")

        PAIRS = B // 4

        def pairs(eng, body):
            if PAIRS == 1:
                body(0, False, False)
            else:
                body(0, False, True)
                if PAIRS > 2:
                    with eng.Fori(1, PAIRS - 1) as i:
                        body(i, True, True)
                body(PAIRS - 1, True, False)

        def state(cyc):
            return 2 - cyc % 2 if cyc else 0

        block = ctx.enter_context(nc.Block())

        small_w = [
            (w_tok[:], a["w_tok"]),
            (tok_add[:, 0, :], a["tok_b"].partition_broadcast(P)),
            (tok_add[:, 1, :], a["tok_b"].partition_broadcast(P)),
            (wk_row[:], a["wk"].partition_broadcast(P)),
            (wq_row[:], a["wq"].partition_broadcast(P)),
            (wdq[:], a["wdq"]), (wuqT[:], a["wuqT"]), (wdkv[:], a["wdkv"]), (wukvT[:], a["wukvT"]),
            (wqr[:], a["wqr"]), (wkr[:], a["wkr"]), (woT[:], a["woT"]),
            (cn_w1[:], a["cn_w1"].rearrange("(t p) m -> p t m", p=P)),
            (cn_w2[:], a["cn_w2"].rearrange("(t p) m -> p t m", p=P)),
            (cn_w3[:], a["cn_w3"]), (cn_w4[:], a["cn_w4"]),
            (cn_b1[:], a["cn_b1"]),
            (cn_b2[:], a["cn_b2"].rearrange("(p o) -> p o", o=1)),
            (cn_b3[:], a["cn_b3"].rearrange("(p o) -> p o", o=1)),
            (cn_b4[:, 0:1], a["cn_b4"].partition_broadcast(P)),
            (gc_w1[:], a["gc_w1"].rearrange("(t p) m -> p t m", p=P)),
            (gc_w2[:], a["gc_w2"]), (gc_w3[:], a["gc_w3"]),
            (gc_b1[:], a["gc_b1"].rearrange("(p o) -> p o", o=1)),
            (gc_b2[:], a["gc_b2"].rearrange("(p o) -> p o", o=1)),
            (gc_b3[:, 0:1], a["gc_b3"].partition_broadcast(P)),
            (ar[:], a["ar"].partition_broadcast(P)),
        ]
        N_CV = 15
        N_W = 16 * (len(small_w) + 1)

        def images(eng, step):
            step(0, 0, True, False, False)
            step(1, 1, True, True, False)
            with eng.Fori(0, B // 2 - 1) as i:
                step(i * 2 + 2, 0, True, True, True)
                step(i * 2 + 3, 1, True, True, True)
            step(B, 0, False, True, True)
            step(B + 1, 1, False, False, True)

        def later(m, n):
            return not isinstance(m, int) or m >= n

        @block.sync
        def _(sp):
            for dst, src in small_w:
                sp.dma_start(dst, src).then_inc(s_w, 16)
            sp.wait_ge(s_w, N_W - 16)
            sp.dma_start(tok_add[0:1, 0, :], a["cls"]).then_inc(s_w, 16)

            def load_x(m, par):
                sp.dma_start(xb[:, par, :, 1:T], a["x"][m]).then_inc(x_loaded[par], 16)

            def store_h1(m, par):
                sp.wait_ge(h1_ready, m * 2 + 1)
                sp.dma_start(h1_dram[m, 0:P, :], h1[:, par, 0, :]).then_inc(h1_stored[par], 16)
                sp.wait_ge(h1_ready, m * 2 + 2)
                sp.dma_start(h1_dram[m, P:T, :], h1[0:T1, par, 1, :]).then_inc(h1_stored[par], 16)

            load_x(0, 0)
            load_x(1, 1)
            sp.wait_ge(s_cv, 1)
            sp.wait_ge(s_pwc, 5)
            for n in range(8):
                sp.dma_start(w_qkv[HD * n:HD * n + HD, :, n, :], small[:, :, :]).then_inc(s_blk, 16)
            with sp.Fori(0, B // 2 - 1) as i:
                for par in range(2):
                    sp.wait_ge(tok_done, i * 4 + 2 * par + 2)
                    load_x(i * 2 + 2 + par, par)
                    store_h1(i * 2 + par, par)
            store_h1(B - 2, 0)
            store_h1(B - 1, 1)
            for par in range(2):
                sp.wait_ge(h1_stored[par], 16 * B + 1)

            def load2(dst, i, c, s):
                for t in range(2):
                    src = h1_dram[:, t * P:t * P + TS[t], :].rearrange("(g n) p d -> g p n d", n=2)
                    sp.dma_start(dst[0:TS[t], c, t, :, :], src[i * 2 + c]).then_inc(s[c], 16)

            for c in range(2):
                load2(hl, 0, c, hl_loaded)
                load2(hk, 0, c, hk_loaded)

            def store_out(i, c):
                for t in range(2):
                    sp.wait_ge(y_ready[c], i * 2 + t + 1)
                    dst = out[:, t * P:t * P + TS[t], :].rearrange("(g n) p d -> g p n d", n=2)
                    sp.dma_start(dst[i * 2 + c], hk[0:TS[t], c, t, :, :]).then_inc(out_stored[c], 16)

            def next_hl(i):
                for c in range(2):
                    sp.wait_ge(hn2_ready[c], i * 4)
                    load2(hl, i, c, hl_loaded)

            def store_and_next_hk(i):
                for c in range(2):
                    store_out(i, c)
                    sp.wait_ge(out_stored[c], i * 32 + 32)
                    load2(hk, i + 1, c, hk_loaded)

            if PAIRS > 1:
                next_hl(1)
                if PAIRS > 2:
                    with sp.Fori(0, PAIRS - 2) as i:
                        next_hl(i + 2)
                        store_and_next_hk(i)
                store_and_next_hk(PAIRS - 2)
            for c in range(2):
                store_out(PAIRS - 1, c)
            for c in range(2):
                sp.wait_ge(out_stored[c], 32 * PAIRS)

        @block.gpsimd
        def _(pool):
            g = nc.gpsimd
            g.memset(ident[:], 0.0).then_inc(s_cp, 1)
            g.memset(mask0[:], 0.0).then_inc(s_cp, 1)
            g.memset(mask1[:], 0.0).then_inc(s_cp, 1)
            g.memset(sign[:], 1.0).then_inc(s_cp, 1)
            g.memset(power[:], -0.5).then_inc(s_cp, 1)
            g.memset(rms_eps[:], RMS_EPS).then_inc(s_cp, 1)
            for par in range(2):
                g.memset(ve[:, par, :], 0.0).then_inc(h1_stored[par], 1)
            pool.wait_ge(s_cp, 6)
            g.affine_select(out=ident[:], in_=ident[:], compare_op=ALU.not_equal, fill=1.0, base=0,
                            pattern=[[-1, P]], channel_multiplier=1).then_inc(s_cp, 1)
            g.affine_select(out=mask0[:], in_=mask0[:], compare_op=ALU.is_ge, fill=NEG, base=0,
                            pattern=[[0, 4], [-1, P]], channel_multiplier=1).then_inc(s_cp, 1)
            g.affine_select(out=mask1[:], in_=mask1[:], compare_op=ALU.is_ge, fill=NEG, base=0,
                            pattern=[[0, 2], [-1, E1]], channel_multiplier=1).then_inc(s_cp, 1)
            g.affine_select(out=sign[:], in_=sign[:], compare_op=ALU.is_ge, fill=-1.0, base=P // 2 - 1,
                            pattern=[[0, 1]], channel_multiplier=-1).then_inc(s_cp, 1)

            def wait(semaphore, value):
                pool.wait_ge(semaphore, value).then_inc(pool_waits, 1)

            def norm(m, t):
                M = TS[t]
                n = m * 2 + t + 1
                wait(mv_ready, n)
                g.tensor_scalar(ve[:M, t, :], mv[:M, t, 1:2], LN_EPS, None, ALU.add).then_inc(ve_done, 1)
                pool.wait_ge(ve_done, n)
                g.tensor_tensor(rstd[:M, t, :], ve[:M, t, :], power[:M, 0:1], ALU.pow).then_inc(rstd_done, 1)

            def select(m, i):
                wait(e_done, m * 12 + 3 * i + 2)
                v = p0[:, i, :, 0:P]
                g.affine_select(out=v, in_=v, compare_op=ALU.is_ge, fill=0.0, base=0,
                                pattern=[[0, HG], [1, P]], channel_multiplier=-1).then_inc(m_done, 1)
                wait(e_done, m * 12 + 3 * i + 3)
                v = p1[:T1, i, :, :]
                g.affine_select(out=v, in_=v, compare_op=ALU.is_ge, fill=0.0, base=0,
                                pattern=[[0, HG], [1, T1]], channel_multiplier=-1).then_inc(m_done, 1)

            def residual(m, par):
                for t in range(2):
                    M = TS[t]
                    pool.wait_ge(att_ready, m * 2 + t + 1)
                    if later(m, 2):
                        pool.wait_ge(h1_stored[par], m * 16 - 16 * par + 1)
                    g.tensor_tensor(h1[:M, par, t, :], h[:M, par, t, :], att[:M, t, :], ALU.add)\
                     .then_inc(h1_ready, 1)

            def step(n, par, new, old, late):
                if late:
                    residual(n - 2, par)
                if new:
                    norm(n, 0)
                    norm(n, 1)
                if old:
                    for i in range(4):
                        select(n - 1, i)

            pool.wait_ge(s_w, N_W)
            images(pool, step)

            def norm2(i, c):
                wait(mv2_ready[c], i * 4 + 4)
                g.tensor_scalar(ve2[:, c, :], mv2[:, c, :, 1], LN_EPS, None, ALU.add).then_inc(ve2_done[c], 1)
                pool.wait_ge(ve2_done[c], i + 1)
                g.tensor_tensor(rstd2[:, c, :], ve2[:, c, :], power[:, 0:4], ALU.pow).then_inc(rstd2_done[c], 1)

            with pool.Fori(0, PAIRS) as i:
                for c in range(2):
                    norm2(i, c)

        @block.scalar
        def _(act):
            s = nc.scalar

            def copy(o, i_):
                return s.activation(o, i_, ACT.Copy)

            def exps(m, i):
                for jj in range(2):
                    act.wait_ge(t_done, m * 12 + 3 * i + jj + 1)
                    s.activation(p0[:, i, 2 * jj:2 * jj + 2, :],
                                 ps[:, TT[jj], 0:2 * TE].rearrange("p (a b) -> p a b", b=TE)[:, :, 0:T],
                                 ACT.Exp).then_inc(e_done, 1)
                act.wait_ge(t_done, m * 12 + 3 * i + 3)
                s.activation(p1[:T1, i, :, :], ps[:T1, TK, 0:4 * E1].rearrange("p (a b) -> p a b", b=E1)[:, :, 0:T1],
                             ACT.Exp).then_inc(e_done, 1)

            def hnT_copy(m, t):
                act.wait_ge(hnT_done, m * 2 + t + 1)
                a, b = t * P, t * P + TS[t]
                copy(hnT[:, :, a:b], ps[:, W[1 - t], 0:N2].rearrange("p (f n) -> p f n", f=FT)[:, :, a:b])\
                    .then_inc(hnT_ready, 1)

            def qkv_copy(m, par, t, f):
                M = TS[t]
                bank = ps[:M, WQ[t][f], :].rearrange("p (s h d) -> p s h d", s=4, d=HD)
                act.wait_ge(qkv_done, m * 4 + 2 * t + f + 1)
                s.activation(sq[:M, t, :, 8 * f:8 * f + 8, :], bank[:, Q:K + 1], ACT.Square).then_inc(sq_ready, 1)
                copy(qkv[:M, par, t, :, 8 * f:8 * f + 8, 0:HD], bank).then_inc(qkv_ready, 1)

            def rms(m, t):
                M = TS[t]
                n = m * 2 + t + 1
                act.wait_ge(ss_ready, n)
                s.activation(ls[:M, t, :], ss[:M, t, :], ACT.Ln, bias=rms_eps[:M, 0:1], scale=1.0 / HD)\
                 .then_inc(ls_ready, 1)
                act.wait_ge(ls_ready, n)
                s.activation(rs[:M, t, :], ls[:M, t, :], ACT.Exp, scale=-0.5).then_inc(rs_ready, 1)

            def q_high_part(m, par, t):
                M = TS[t]
                act.wait_ge(qk_normed, m * 2 + t + 1)
                x_ = qkv[:M, par, t, Q, :, 0:HD].rearrange("p h (o d) -> p h o d", o=1)
                copy(q2[:M, t, :, 0:3:2, :], x_.to_broadcast([M, H, 2, HD])).then_inc(q_high, 1)

            def qkT_copy(m):
                for b in range(4):
                    act.wait_ge(qk_transposed, m * 8 + (1, 2, 5, 6)[b])
                    copy(qT[:, 2 * b:2 * b + 2, :], ps[:, QB[b], 0:2 * TE].rearrange("p (a b) -> p a b", b=TE))\
                        .then_inc(qT_ready, 1)
                for b in range(2, 4):
                    act.wait_ge(qk_transposed, m * 8 + 5 + b)
                    copy(kT[:, 2 * b:2 * b + 2, :], ps[:, KB[b], 0:2 * TE].rearrange("p (a b) -> p a b", b=TE))\
                        .then_inc(kT_ready, 1)

            def ctx1(m):
                act.wait_ge(pv_done, m * 2 + 2)
                copy(ctxT[:, 2:4, :], ps[:, W[0], 0:N2].rearrange("p (a b) -> p a b", b=T))\
                    .then_inc(ctx1_ready, 1)

            def step(n, par, new, old, late):
                if late:
                    ctx1(n - 2)
                if old:
                    qkT_copy(n - 1)
                if new:
                    hnT_copy(n, 0)
                    qkv_copy(n, par, 0, 0)
                    qkv_copy(n, par, 0, 1)
                if old:
                    exps(n - 1, 0)
                if new:
                    hnT_copy(n, 1)
                    rms(n, 0)
                if old:
                    exps(n - 1, 1)
                if new:
                    qkv_copy(n, par, 1, 0)
                if old:
                    exps(n - 1, 2)
                if new:
                    qkv_copy(n, par, 1, 1)
                    rms(n, 1)
                    q_high_part(n, par, 0)
                if old:
                    exps(n - 1, 3)
                if new:
                    q_high_part(n, par, 1)

            s.add_instruction(mybir.InstLoadActFuncSet(name=nc.get_next_instruction_name(), ins=[], outs=[],
                                                       engine=s.engine, act_func_set_id=LN_EXP_SET))
            act.wait_ge(s_cv, N_CV)
            act.wait_ge(s_cp, 10)
            images(act, step)

            def x_copy(i, c):
                for f in range(FT):
                    act.wait_ge(x_done[c], i * 2 + f + 1)
                    copy(X[:, c, 0, f, :], ps[:, 4 * c + f, 0:N2]).then_inc(x_ready[c], 1)

            def gnet(i, c, l):
                act.wait_ge(g_done[c], i * 3 + l + 1)
                if l == 0:
                    s.activation(ga1[:, c, :], ps[:G1, 4 * c + 3, 0:2], ACT.Gelu, bias=gc_b1[:, 0:1],
                                 scale=1.0 / T).then_inc(g_ready[c], 1)
                elif l == 1:
                    s.activation(ga2[:, c, :], ps[:G2, 4 * c + 3, 0:2], ACT.Gelu, bias=gc_b2[:, 0:1])\
                     .then_inc(g_ready[c], 1)
                else:
                    s.activation(gth[:, c, :], ps[:, 4 * c + 3, 0:2], ACT.Tanh, bias=gc_b3[:, 1:2], scale=0.5)\
                     .then_inc(g_ready[c], 1)

            def layer(i, c, cyc, l):
                n = (i * CYCLES + cyc) * 5
                if l == 0:
                    for mt in range(2):
                        act.wait_ge(l_done[c], n + mt + 1)
                        s.activation(a1[:, c, mt, :], ps[:, 4 * c + mt, 0:N2], ACT.Gelu,
                                     bias=cn_b1[:, mt:mt + 1]).then_inc(l_ready[c], 1)
                elif l == 1:
                    act.wait_ge(l_done[c], n + 3)
                    s.activation(a2[:, c, :], ps[:, 4 * c + 2, 0:N2], ACT.Gelu, bias=cn_b2[:, 0:1])\
                     .then_inc(l_ready[c], 1)
                elif l == 2:
                    act.wait_ge(l_done[c], n + 4)
                    s.activation(a3[:, c, :], ps[:F3, 4 * c + 3, 0:N2], ACT.Gelu, bias=cn_b3[:, 0:1])\
                     .then_inc(l_ready[c], 1)
                else:
                    act.wait_ge(l_done[c], n + 5)
                    s.activation(th[:, c, :], ps[:, 4 * c + 2, 0:N2], ACT.Tanh, bias=cn_b4[:, 1:2], scale=0.5)\
                     .then_inc(l_ready[c], 1)

            def pass2(i, prev, nxt):
                for cyc in range(CYCLES):
                    last = nxt and cyc == CYCLES - 1
                    layer(i, 0, cyc, 0)
                    if last:
                        gnet(i + 1, 0, 0)
                    if cyc == 0 and prev:
                        gnet(i, 1, 2)
                    if cyc or prev:
                        layer(i if cyc else i - 1, 1, (cyc - 1) % CYCLES, 2)
                    layer(i, 0, cyc, 1)
                    if cyc or prev:
                        layer(i if cyc else i - 1, 1, (cyc - 1) % CYCLES, 3)
                    layer(i, 0, cyc, 2)
                    layer(i, 0, cyc, 3)
                    if nxt and cyc == 1:
                        x_copy(i + 1, 0)
                    if last:
                        gnet(i + 1, 0, 1)
                    layer(i, 1, cyc, 0)
                    if last:
                        gnet(i + 1, 1, 0)
                    layer(i, 1, cyc, 1)
                    if nxt and cyc == 1:
                        x_copy(i + 1, 1)
                    if last:
                        gnet(i + 1, 0, 2)
                        gnet(i + 1, 1, 1)

            for c in range(2):
                x_copy(0, c)
            for l in range(3):
                for c in range(2):
                    gnet(0, c, l)
            pairs(act, pass2)
            layer(PAIRS - 1, 1, CYCLES - 1, 2)
            layer(PAIRS - 1, 1, CYCLES - 1, 3)

        @block.vector
        def _(dve):
            v = nc.vector
            v.memset(w_qkv[:], 0.0).then_inc(s_cv, 1)
            v.memset(qkv[:], 0.0).then_inc(s_cv, 1)
            v.memset(xb[:, :, :, 0:1], 0.0).then_inc(s_cv, 1)
            v.memset(mxT[:].bitcast(F32), 0.0).then_inc(s_cv, 1)
            v.memset(q2[:].bitcast(F32), 0.0).then_inc(s_cv, 1)
            v.memset(k2[:].bitcast(F32), 0.0).then_inc(s_cv, 1)
            dve.wait_ge(s_cv, 2)
            v.memset(qkv[:, :, :, V, :, HD:HD + 1].rearrange("p a t h o -> p (a t) h o"), 1.0).then_inc(s_cv, 1)
            dve.wait_ge(s_w, N_W)
            v.tensor_scalar(wq_row[:], wq_row[:], float(HD) ** -0.5, None, ALU.mult).then_inc(s_cv, 1)
            dve.wait_ge(s_cv, 8)
            v.tensor_tensor(wk_row[:], wk_row[:], wq_row[:], ALU.mult).then_inc(s_cv, 1)
            dve.wait_ge(s_cp, 10)
            v.memset(mv2[:], 1.0).then_inc(s_cv, 1)
            v.tensor_copy(ident_b[:], ident[:]).then_inc(s_cv, 1)
            v.tensor_copy(ident_r[:], ident[:]).then_inc(s_cv, 1)
            v.tensor_copy(cn_w4r[:], cn_w4[:, 0:1].to_broadcast([F3, P]))
            v.tensor_copy(gc_w3r[:], gc_w3[:, 0:1].to_broadcast([G2, P]))
            v.tensor_scalar(cn_b4[:, 1:2], cn_b4[:, 0:1], 0.5, None, ALU.mult)
            v.tensor_scalar(gc_b3[:, 1:2], gc_b3[:, 0:1], 0.5, None, ALU.mult)
            v.tensor_scalar(c_tf[:], sign[:], ar[:, 0:1], 0.3, ALU.mult, ALU.mult).then_inc(s_cv, 1)
            v.tensor_scalar(c_gf[:], sign[:], ar[:, 0:1], 0.7, ALU.mult, ALU.mult).then_inc(s_cv, 1)
            v.tensor_scalar(c_base[:], sign[:], 0.1, None, ALU.mult).then_inc(s_cv, 1)
            dve.wait_ge(s_pw, 4)
            v.tensor_copy(small[:, Q, :], ps[:HD, 0, 0:HD]).then_inc(s_pwc, 1)
            v.tensor_copy(small[:, K, :], ps[:HD, 1, 0:HD]).then_inc(s_pwc, 1)
            v.tensor_copy(a_v[:], ps[:HD, 2, 0:HD]).then_inc(s_pwc, 1)
            v.tensor_tensor(small[:, R, :], ps[:HD, 3, 0:HD], wq_row[:HD, :], ALU.mult).then_inc(s_pwc, 1)
            dve.wait_ge(s_pw, 5)
            v.tensor_copy(small[:, V, :], ps[:HD, 4, 0:HD]).then_inc(s_pwc, 1)

            def embed(m, par, t):
                M = TS[t]
                dve.wait_ge(tok_done, m * 2 + t + 1)
                if later(m, 2):
                    dve.wait_ge(h1_ready, m * 2 + t - 3)
                v.tensor_tensor(h[:M, par, t, :], ps[:M, TOK[t], 0:D], tok_add[:M, t, :], ALU.add)\
                 .then_inc(h_ready, 1)

            def stats(m, par, t):
                M = TS[t]
                n = m * 2 + t + 1
                dve.wait_ge(h_ready, n)
                v.bn_stats(st[:M, t, :], h[:M, par, t, :]).then_inc(bn_done, 1)
                dve.wait_ge(bn_done, n).then_inc(dve_waits, 1)
                v.bn_aggr(mv[:M, t, :], st[:M, t, :]).then_inc(mv_ready, 1)

            def hn_apply(m, par, t):
                M = TS[t]
                dve.wait_ge(rstd_done, m * 2 + t + 1)
                v.tensor_scalar(hn[:M, t, :], h[:M, par, t, :], mv[:M, t, 0:1], rstd[:M, t, :],
                                ALU.subtract, ALU.mult).then_inc(hn_ready, 1)

            def mxT_copy(m):
                dve.wait_ge(mx_transposed, m + 1)
                v.tensor_copy(mxT[:H, 0:T], ps[:H, SA, 0:T]).then_inc(mxT_ready, 1)

            def rms_sum(m, t):
                M = TS[t]
                dve.wait_ge(sq_ready, m * 4 + 2 * t + 2)
                v.tensor_reduce(ss[:M, t, :], sq[:M, t].rearrange("p s h d -> p (s h) d"), AX.X, ALU.add)\
                 .then_inc(ss_ready, 1)

            def rms_mul(m, par, t):
                M = TS[t]
                n = m * 2 + t + 1
                dve.wait_ge(ss_ready, n)
                v.tensor_scalar(xh[:M, t, :], ss[:M, t, :], -0.5 / HD, -0.5 * RMS_EPS, ALU.mult, ALU.add)\
                 .then_inc(xh_ready, 1)
                dve.wait_ge(rs_ready, n)
                y = rs[:M, t, :]
                v.tensor_tensor(y2[:M, t, :], y, y, ALU.mult).then_inc(y2_ready, 1)
                dve.wait_ge(xh_ready, n)
                dve.wait_ge(y2_ready, n)
                v.tensor_tensor(y2[:M, t, :], y2[:M, t, :], xh[:M, t, :], ALU.mult).then_inc(y2x_ready, 1)
                dve.wait_ge(y2x_ready, n)
                v.scalar_tensor_tensor(rms[:M, t, :], y2[:M, t, :], 1.5, y, ALU.add, ALU.mult)\
                 .then_inc(rms_ready, 1)
                dve.wait_ge(rms_ready, n)
                qk = qkv[:M, par, t, Q:K + 1, :, 0:HD]
                r = rms[:M, t, :].rearrange("p (s h o) -> p s h o", s=2, o=1).to_broadcast([M, 2, H, HD])
                v.tensor_tensor(qk, qk, r, ALU.mult).then_inc(qk_normed, 1)

            def k_sum(m, par, t):
                M = TS[t]
                n = m * 2 + t + 1
                dve.wait_ge(qk_normed, n)
                k = qkv[:M, par, t, K, :, 0:HD]
                wk = wk_row[:M, :].rearrange("p (o d) -> p o d", o=1).to_broadcast([M, H, HD])
                v.tensor_tensor(k, k, wk, ALU.mult).then_inc(kw_done, 1)
                dve.wait_ge(kw_done, n)
                v.tensor_tensor(k, k, qkv[:M, par, t, R, :, 0:HD], ALU.add).then_inc(k_ready, 1)
                dve.wait_ge(k_ready, n)
                k4 = k.rearrange("p h (o d) -> p h o d", o=1).to_broadcast([M, H, 2, HD])
                v.tensor_copy(k2[:M, t, :, 0:2, :], k4).then_inc(k_high, 1)
                dve.wait_ge(k_high, n)
                v.tensor_tensor(k2[:M, t, :, 2, :], k, k2[:M, t, :, 0, :].bitcast(F32), ALU.subtract)\
                 .then_inc(k2_ready, 1)

            def q_low_part(m, par, t):
                M = TS[t]
                dve.wait_ge(q_high, m * 2 + t + 1)
                v.tensor_tensor(q2[:M, t, :, 1, :], qkv[:M, par, t, Q, :, 0:HD], q2[:M, t, :, 0, :].bitcast(F32),
                                ALU.subtract).then_inc(q2_ready, 1)

            def ctx0(m):
                dve.wait_ge(pv_done, m * 2 + 1)
                v.tensor_copy(ctxT[:, 0:2, :], ps[:, W[1], 0:N2].rearrange("p (a b) -> p a b", b=T))\
                 .then_inc(ctx0_ready, 1)

            def kT_copy(m):
                for b in range(2):
                    dve.wait_ge(qk_transposed, m * 8 + 3 + b)
                    v.tensor_copy(kT[:, 2 * b:2 * b + 2, :], ps[:, KB[b], 0:2 * TE].rearrange("p (a b) -> p a b", b=TE))\
                     .then_inc(kT_ready, 1)

            def attend(m):
                for t in range(2):
                    M = TS[t]
                    c = ps[:M, TT[t], :].rearrange("p (h d) -> p h d", d=SLOT)
                    dve.wait_ge(ctx_transposed, m * 2 + t + 1)
                    v.reciprocal(rden[:M, t, :], c[:, :, HD]).then_inc(rden_done, 1)
                    dve.wait_ge(rden_done, m * 2 + t + 1)
                    if isinstance(m, int):
                        dve.wait_ge(h1_ready, m * 2 + t - 1)
                    r = rden[:M, t, :].rearrange("p (h o) -> p h o", o=1).to_broadcast([M, H, HD])
                    v.tensor_tensor(att[:M, t, :].rearrange("p (h d) -> p h d", d=HD), c[:, :, 0:HD], r,
                                    ALU.mult).then_inc(att_ready, 1)

            def maxima(m, i):
                n = m * 12 + 3 * i
                dve.wait_ge(s_done, n + 1)
                v.tensor_reduce(mx[:, 0, head(i, 0)[2]:head(i, 3)[2] + 1:2], ps[:, SA, :].rearrange("p (a b) -> p a b", b=P),
                                AX.X, ALU.max, negate=True).then_inc(s_max, 1)
                for jj in range(2):
                    dve.wait_ge(s_done, n + 2 + jj)
                    v.tensor_reduce(mx[:T1, 1, head(i, 2 * jj)[2]:head(i, 2 * jj + 1)[2] + 1:2],
                                    ps[:T1, SB[jj], 0:2 * TE].rearrange("p (a b) -> p a b", b=TE),
                                    AX.X, ALU.max, negate=True).then_inc(s_max, 1)

            def step(n, par, new, old, late):
                if late:
                    attend(n - 2)
                if old:
                    kT_copy(n - 1)
                if new:
                    embed(n, par, 0)
                    stats(n, par, 0)
                if old:
                    maxima(n - 1, 0)
                if new:
                    hn_apply(n, par, 0)
                if old:
                    maxima(n - 1, 1)
                if new:
                    embed(n, par, 1)
                if old:
                    maxima(n - 1, 2)
                    maxima(n - 1, 3)
                if new:
                    stats(n, par, 1)
                if old:
                    mxT_copy(n - 1)
                if new:
                    hn_apply(n, par, 1)
                    rms_sum(n, 0)
                    rms_mul(n, par, 0)
                    k_sum(n, par, 0)
                    rms_sum(n, 1)
                if old:
                    ctx0(n - 1)
                if new:
                    rms_mul(n, par, 1)
                    k_sum(n, par, 1)
                    q_low_part(n, par, 0)
                    q_low_part(n, par, 1)

            images(dve, step)

            def stats2(i, c):
                dve.wait_ge(hl_loaded[c], i * 32 + 32)
                for k in range(4):
                    t, n = divmod(k, 2)
                    v.bn_stats(st2[:TS[t], c, k, :], hl[:TS[t], c, t, n, :]).then_inc(bn2_done[c], 1)
                dve.wait_ge(bn2_done[c], i * 4 + 4).then_inc(dve_waits, 1)
                for k in range(4):
                    M = TS[k // 2]
                    v.bn_aggr(mv2[:M, c, k, :], st2[:M, c, k, :]).then_inc(mv2_ready[c], 1)

            def apply2(i, c, first):
                dve.wait_ge(rstd2_done[c], i + 1)
                if not first:
                    dve.wait_ge(x_done[c], i * 2)
                for k in range(4):
                    t, n = divmod(k, 2)
                    M = TS[t]
                    v.tensor_scalar(hn2[:M, c, k, :], hl[:M, c, t, n, :], mv2[:M, c, k, 0:1],
                                    rstd2[:M, c, k:k + 1], ALU.subtract, ALU.mult).then_inc(hn2_ready[c], 1)

            def gsums(i, c):
                dve.wait_ge(x_ready[c], i * 2 + 2)
                v.tensor_reduce(gsum[:, c, :, :], X[:, c, 0, :, :].rearrange("p f (n t) -> p (f n) t", t=T), AX.X,
                                ALU.add).then_inc(gsum_ready[c], 1)

            def alphas(i, c):
                dve.wait_ge(g_ready[c], i * 3 + 3)
                v.tensor_scalar(alpha[:, c, :], gth[:, c, :], c_gf[:, 0:1], c_base[:, 0:1], ALU.mult, ALU.add)\
                 .then_inc(alpha_ready[c], 1)

            def update(i, c, cyc, first):
                n = i * CYCLES + cyc + 1
                old, new = X[:, c, state(cyc)], X[:, c, state(cyc + 1)]
                dve.wait_ge(alpha_ready[c], i + 1)
                for f, op in ((0, ALU.add), (1, ALU.subtract)):
                    for im in range(2):
                        cols = slice(im * T, im * T + T)
                        v.scalar_tensor_tensor(base[:, c, f, cols], old[:, 1 - f, cols],
                                               alpha[:, c, im:im + 1], old[:, f, cols], ALU.mult, op)\
                         .then_inc(base_ready[c], 1)
                dve.wait_ge(l_ready[c], n * 5)
                v.scalar_tensor_tensor(u0[:, c, :], old[:, 1, :], c_tf[:, 0:1], th[:, c, :], ALU.mult, ALU.mult)\
                 .then_inc(u0_ready[c], 1)
                if cyc == 0 and not first:
                    dve.wait_ge(y_done[c], i * 2)
                dve.wait_ge(base_ready[c], n * 4)
                dve.wait_ge(u0_ready[c], n)
                v.tensor_tensor(new[:, 0, :], base[:, c, 0, :], u0[:, c, :], ALU.add).then_inc(x0_new[c], 1)
                v.scalar_tensor_tensor(u1[:, c, :], old[:, 0, :], c_tf[:, 0:1], th[:, c, :], ALU.mult, ALU.mult)\
                 .then_inc(u1_ready[c], 1)
                dve.wait_ge(u1_ready[c], n)
                v.scalar_tensor_tensor(new[:, 1, :], base[:, c, 1, :], -1.0, u1[:, c, :], ALU.mult, ALU.subtract)\
                 .then_inc(x1_new[c], 1)

            def finish(i, c):
                dve.wait_ge(hk_loaded[c], i * 32 + 32)
                for t in range(2):
                    M = TS[t]
                    dve.wait_ge(y_done[c], i * 2 + t + 1)
                    y = hk[:M, c, t, :, :]
                    v.tensor_tensor(y, y, ps[:M, 4 * c + 2 + t, :].rearrange("p (n d) -> p n d", n=2), ALU.add)\
                     .then_inc(y_ready[c], 1)

            def pass2(i, prev, nxt):
                if prev:
                    finish(i - 1, 0)
                    update(i - 1, 1, CYCLES - 1, False)
                    alphas(i, 1)
                    finish(i - 1, 1)
                update(i, 0, 0, not prev)
                if nxt:
                    stats2(i + 1, 0)
                    stats2(i + 1, 1)
                    apply2(i + 1, 0, False)
                update(i, 1, 0, not prev)
                if nxt:
                    apply2(i + 1, 1, False)
                update(i, 0, 1, False)
                if nxt:
                    gsums(i + 1, 0)
                update(i, 1, 1, False)
                if nxt:
                    gsums(i + 1, 1)
                update(i, 0, 2, False)
                if nxt:
                    alphas(i + 1, 0)

            for c in range(2):
                stats2(0, c)
            for c in range(2):
                apply2(0, c, True)
            for c in range(2):
                gsums(0, c)
            for c in range(2):
                alphas(0, c)
            pairs(dve, pass2)
            finish(PAIRS - 1, 0)
            update(PAIRS - 1, 1, CYCLES - 1, False)
            finish(PAIRS - 1, 1)

        @block.tensor
        def _(pe):
            t_ = nc.tensor
            pe.wait_ge(s_w, N_W)
            t_.matmul(ps[:HD, 0, 0:HD], wdq[:], wuqT[:], start=True, stop=True).then_inc(s_pw, 1)
            for c in range(2):
                mm = t_.matmul(ps[:HD, 1, 0:HD], wdkv[:, c, :], wukvT[:, c, 0:HD], start=c == 0, stop=c == 1)
            mm.then_inc(s_pw, 1)
            for c in range(2):
                mm = t_.matmul(ps[:HD, 2, 0:HD], wukvT[:, c, HD:2 * HD], wdkv[:, c, :], start=c == 0, stop=c == 1)
            mm.then_inc(s_pw, 1)
            t_.matmul(ps[:HD, 3, 0:HD], wkr[:], wqr[:], start=True, stop=True).then_inc(s_pw, 1)
            pe.wait_ge(s_pwc, 3)
            t_.matmul(ps[:HD, 4, 0:HD], a_v[:], woT[:], start=True, stop=True).then_inc(s_pw, 1)
            pe.wait_ge(s_cv, N_CV)
            pe.wait_ge(s_pwc, 5)
            pe.wait_ge(s_cp, 10)

            def tok(m, par, t, ks=None):
                M = TS[t]
                for k in range(KT) if ks is None else ks:
                    mm = t_.matmul(ps[:M, TOK[t], 0:D], xb[:, par, k, t * P:t * P + M], w_tok[:, k, :],
                                   start=k == 0, stop=k == KT - 1)
                if ks is None or KT - 1 in ks:
                    mm.then_inc(tok_done, 1)

            def mx_transpose(m):
                for t in range(2):
                    M = TS[t]
                    mm = t_.transpose(ps[:H, SA, t * P:t * P + M], mx[:M, t, :], ident[:M, :M])
                mm.then_inc(mx_transposed, 1)

            def hn_transpose(m, t):
                M = TS[t]
                pe.wait_ge(hn_ready, m * 2 + t + 1)
                for f in range(FT):
                    mm = t_.transpose(ps[:, W[1 - t], f * T + t * P:f * T + t * P + M],
                                      hn[:M, t, f * P:f * P + P], ident[:M, :M])
                mm.then_inc(hnT_done, 1)

            def project(m, t, f):
                M = TS[t]
                t_.matmul(ps[:M, WQ[t][f], :], hnT[:, f, t * P:t * P + M],
                          w_qkv[:].rearrange("p s h d -> p (s h d)"), start=True, stop=True).then_inc(qkv_done, 1)

            def scoresT(m, i):
                n = m * 12 + 3 * i
                again = i > 0 or later(m, 1)

                def products(b, ks, width, keys, queries):
                    M = keys.stop - keys.start
                    for x_, k in enumerate(ks):
                        rows, j, h = head(i, k)
                        t_.matmul(ps[:M, b, x_ * width:x_ * width + width], kT[rows, j, keys], qT[rows, j, queries],
                                  start=x_ == 0, stop=False)

                def less_max(b, ks, width, keys, queries):
                    M = keys.stop - keys.start
                    for x_, k in enumerate(ks):
                        rows, j, h = head(i, k)
                        mm = t_.matmul(ps[:M, b, x_ * width:x_ * width + width],
                                       ident_r[:, h:h + 1].to_broadcast([P, M]), mxT[:, queries],
                                       start=False, stop=k == ks[-1])
                    mm.then_inc(t_done, 1)

                first = [(TT[jj], (2 * jj, 2 * jj + 1), TE, slice(0, P), slice(0, TE)) for jj in range(2)]
                second = TK, range(4), E1, slice(P, T), slice(P, TE)
                for jj in range(2):
                    if again:
                        pe.wait_ge(e_done, n - 2 + jj)
                    products(*first[jj])
                if i == 0:
                    pe.wait_ge(mxT_ready, m + 1)
                for jj in range(2):
                    less_max(*first[jj])
                if again:
                    pe.wait_ge(e_done, n)
                products(*second)
                less_max(*second)

            def pv(m, par, jj):
                pe.wait_ge(m_done, m * 8 + 4 * jj + 4)
                for j2 in range(2):
                    j = 2 * jj + j2
                    for i in range(4):
                        t_.matmul(ps[SLOT * i:SLOT * i + SLOT, W[1 - jj], j2 * T:j2 * T + T],
                                  qkv[:, par, 0, V, 4 * j + i, :], p0[:, j // 2 * 2 + i % 2, (4 * j + i) % 8 // 2, :], start=True, stop=False,
                                  tile_position=(0, SLOT * i))
                    for i in range(4):
                        mm = t_.matmul(ps[SLOT * i:SLOT * i + SLOT, W[1 - jj], j2 * T + P:j2 * T + T],
                                       qkv[:T1, par, 1, V, 4 * j + i, :], p1[:T1, j // 2 * 2 + i % 2, (4 * j + i) % 8 // 2, :], start=False, stop=True,
                                       tile_position=(0, SLOT * i))
                mm.then_inc(pv_done, 1)

            def qk_transpose(x2, banks, b):
                for j2 in range(2):
                    h = 2 * (2 * b + j2)
                    for t in range(2):
                        M = (P, E1)[t]
                        mm = t_.transpose(ps[:, banks[b], j2 * TE + t * P:j2 * TE + t * P + M].bitcast(F32R),
                                          x2[:M, t, h:h + 2, :, :].rearrange("p h s d -> p (h s d)"),
                                          ident_r[:M, :M])
                mm.then_inc(qk_transposed, 1)

            def ctx_transpose(m, t):
                M = TS[t]
                for j in range(4):
                    mm = t_.transpose(ps[:M, TT[t], j * P:j * P + P], ctxT[:, j, t * P:t * P + M], ident[:, :])
                mm.then_inc(ctx_transposed, 1)

            def scores(m, i):
                n = m * 12 + 3 * i
                if i > 0:
                    pe.wait_ge(s_max, n - 2)
                for k in range(4):
                    rows, j, h = head(i, k)
                    t_.matmul(ps[:, SA, k * P:k * P + P], qT[rows, j, 0:P], kT[rows, j, 0:P],
                              start=k == 0, stop=False)
                t_.matmul(ps[:, SA, :], ident_b[:], mask0[:].rearrange("p a b -> p (a b)"), start=False, stop=True)\
                  .then_inc(s_done, 1)
                for jj in range(2):
                    if i > 0:
                        pe.wait_ge(s_max, n - 1 + jj)
                    bank = ps[:T1, SB[jj], 0:2 * TE].rearrange("p (a b) -> p a b", b=TE)
                    for x_ in range(2):
                        rows, j, h = head(i, 2 * jj + x_)
                        t_.matmul(bank[:, x_, :], qT[rows, j, P:T], kT[rows, j, :], start=x_ == 0, stop=False)
                    t_.matmul(bank[:, :, P:TE], ident_b[:T1, :T1], mask1[:T1], start=False, stop=True)\
                      .then_inc(s_done, 1)

            cuts = (0, 3, 3, 4, 5, KT)
            TOK0 = [range(x, y) for x, y in zip(cuts, cuts[1:])]

            def step(n, par, new, old, late):
                o, opar = n - 1, 1 - par
                if new:
                    pe.wait_ge(x_loaded[par], n * 8 + 16 - 8 * par)
                    if later(n, 1):
                        pe.wait_ge(h_ready, n * 2 - 1)
                    if late:
                        pe.wait_ge(mxT_ready, n - 1)
                    tok(n, par, 0, TOK0[0])
                if late:
                    if old:
                        pe.wait_ge(qkv_ready, n * 4)
                    pv(n - 2, par, 1)
                if old:
                    if not late:
                        pe.wait_ge(qkv_ready, n * 4)
                    pe.wait_ge(q2_ready, o * 2 + 2)
                    qk_transpose(q2, QB, 0)
                    if late:
                        pe.wait_ge(ctx0_ready, n - 1)
                    qk_transpose(q2, QB, 1)
                if new:
                    tok(n, par, 0, TOK0[1])
                if late:
                    pe.wait_ge(ctx0_ready, n - 1)
                    pe.wait_ge(ctx1_ready, n - 1)
                    ctx_transpose(n - 2, 0)
                    ctx_transpose(n - 2, 1)
                if old:
                    pe.wait_ge(k2_ready, o * 2 + 2)
                    qk_transpose(k2, KB, 0)
                    qk_transpose(k2, KB, 1)
                if new:
                    tok(n, par, 0, TOK0[2])
                if old:
                    if late:
                        pe.wait_ge(att_ready, o * 2)
                    qk_transpose(q2, QB, 2)
                    qk_transpose(q2, QB, 3)
                if new:
                    tok(n, par, 0, TOK0[3])
                if old:
                    pe.wait_ge(qT_ready, o * 4 + 1)
                    qk_transpose(k2, KB, 2)
                    qk_transpose(k2, KB, 3)
                if new:
                    tok(n, par, 0, TOK0[4])
                if old:
                    pe.wait_ge(qT_ready, o * 4 + 4)
                    pe.wait_ge(kT_ready, o * 4 + 4)
                for i in range(4):
                    if new and i < 3:
                        tok(n, par, 1, range(i * KT // 3, (i + 1) * KT // 3))
                    if new and i == 0:
                        pe.wait_ge(h_ready, n * 2 + 1)
                    if new and i == 3:
                        hn_transpose(n, 0)
                    if old:
                        scores(o, i)
                if new:
                    if not old:
                        pe.wait_ge(s_blk, 128)
                    pe.wait_ge(h_ready, n * 2 + 2)
                    pe.wait_ge(hnT_ready, n * 2 + 1)
                    project(n, 0, 0)
                    project(n, 0, 1)
                if old:
                    pe.wait_ge(s_max, o * 12 + 12)
                    mx_transpose(o)
                    scoresT(o, 0)
                if new:
                    pe.wait_ge(qkv_ready, n * 4 + 1)
                    hn_transpose(n, 1)
                if old:
                    scoresT(o, 1)
                if new:
                    pe.wait_ge(hnT_ready, n * 2 + 2)
                    pe.wait_ge(qkv_ready, n * 4 + 2)
                    project(n, 1, 0)
                if old:
                    scoresT(o, 2)
                if new:
                    project(n, 1, 1)
                if old:
                    if new:
                        pe.wait_ge(qkv_ready, n * 4 + 3)
                    pv(o, opar, 0)
                    scoresT(o, 3)

            images(pe, step)

            def x_transpose(i, c):
                pe.wait_ge(hn2_ready[c], i * 4 + 4)
                for f in range(FT):
                    for k in range(4):
                        t, n = divmod(k, 2)
                        M = TS[t]
                        mm = t_.transpose(ps[:, 4 * c + f, n * T + t * P:n * T + t * P + M],
                                          hn2[:M, c, k, f * P:f * P + P], ident[:M, :M])
                    mm.then_inc(x_done[c], 1)

            def gnet(i, c, l):
                b = 4 * c + 3
                if l == 0:
                    pe.wait_ge(gsum_ready[c], i + 1)
                    for f in range(FT):
                        mm = t_.matmul(ps[:G1, b, 0:2], gc_w1[:, f, :], gsum[:, c, f, :], start=f == 0,
                                       stop=f == FT - 1)
                else:
                    pe.wait_ge(g_ready[c], i * 3 + l)
                    mm = t_.matmul(ps[:G2, b, 0:2], gc_w2[:], ga1[:, c, :], start=True, stop=True) if l == 1 else \
                        t_.matmul(ps[:, b, 0:2], gc_w3r[:], ga2[:, c, :], start=True, stop=True)
                mm.then_inc(g_done[c], 1)

            def layer(i, c, cyc, l, prev=True, nxt=True):
                n = (i * CYCLES + cyc) * 5
                last = cyc == CYCLES - 1
                if l == 0:
                    if last and nxt:
                        pe.wait_ge(x_ready[c], i * 2 + 4)
                    for f in range(FT):
                        if cyc:
                            pe.wait_ge((x0_new, x1_new)[f][c], i * CYCLES + cyc)
                        elif f == 0:
                            pe.wait_ge(x_ready[c], i * 2 + 2)
                        for mt in range(2):
                            mm = t_.matmul(ps[:, 4 * c + mt, 0:N2], cn_w1[:, f, mt * P:mt * P + P],
                                           X[:, c, state(cyc), f, :], start=f == 0, stop=f == FT - 1)
                            if f == FT - 1:
                                mm.then_inc(l_done[c], 1)
                elif l == 1:
                    if cyc == 0 and prev:
                        pe.wait_ge(y_ready[c], i * 2)
                    for f in range(2):
                        pe.wait_ge(l_ready[c], n + f + 1)
                        mm = t_.matmul(ps[:, 4 * c + 2, 0:N2], cn_w2[:, f, :], a1[:, c, f, :], start=f == 0, stop=f == 1)
                    mm.then_inc(l_done[c], 1)
                elif l == 2:
                    pe.wait_ge(l_ready[c], n + 3)
                    pe.wait_ge(g_ready[c], i * 3 + 6 if last and nxt and c else i * 3 + 4 if last and nxt else i * 3 + 3)
                    t_.matmul(ps[:F3, 4 * c + 3, 0:N2], cn_w3[:], a2[:, c, :], start=True, stop=True)\
                      .then_inc(l_done[c], 1)
                else:
                    pe.wait_ge(l_ready[c], n + 4)
                    t_.matmul(ps[:, 4 * c + 2, 0:N2], cn_w4r[:], a3[:, c, :], start=True, stop=True)\
                      .then_inc(l_done[c], 1)

            def y_transpose(i, c, nxt):
                pe.wait_ge(x0_new[c], i * CYCLES + CYCLES)
                pe.wait_ge(x1_new[c], i * CYCLES + CYCLES)
                if nxt:
                    pe.wait_ge(g_ready[c], i * 3 + 6)
                for t in range(2):
                    M = TS[t]
                    for n in range(2):
                        for f in range(FT):
                            mm = t_.transpose(ps[:M, 4 * c + 2 + t, n * D + f * P:n * D + f * P + P],
                                              X[:, c, state(CYCLES), f, n * T + t * P:n * T + t * P + M], ident[:, :])
                    mm.then_inc(y_done[c], 1)

            def pass2(i, prev, nxt):
                for cyc in range(CYCLES):
                    last = nxt and cyc == CYCLES - 1
                    layer(i, 0, cyc, 0, prev, nxt)
                    if last:
                        gnet(i + 1, 0, 0)
                    if cyc == 0 and prev:
                        gnet(i, 1, 2)
                        y_transpose(i - 1, 0, True)
                    if cyc or prev:
                        layer(i if cyc else i - 1, 1, (cyc - 1) % CYCLES, 2)
                    layer(i, 0, cyc, 1, prev)
                    if cyc or prev:
                        layer(i if cyc else i - 1, 1, (cyc - 1) % CYCLES, 3)
                    layer(i, 0, cyc, 2, prev, nxt)
                    layer(i, 0, cyc, 3)
                    if nxt and cyc == 1:
                        x_transpose(i + 1, 0)
                    if last:
                        gnet(i + 1, 0, 1)
                    if cyc == 0 and prev:
                        y_transpose(i - 1, 1, True)
                    layer(i, 1, cyc, 0, prev, nxt)
                    if last:
                        gnet(i + 1, 1, 0)
                    layer(i, 1, cyc, 1, prev)
                    if nxt and cyc == 1:
                        x_transpose(i + 1, 1)
                    if last:
                        gnet(i + 1, 0, 2)
                        gnet(i + 1, 1, 1)

            for c in range(2):
                x_transpose(0, c)
            for l in range(3):
                for c in range(2):
                    gnet(0, c, l)
            pairs(pe, pass2)
            y_transpose(PAIRS - 1, 0, False)
            layer(PAIRS - 1, 1, CYCLES - 1, 2, nxt=False)
            layer(PAIRS - 1, 1, CYCLES - 1, 3)
            y_transpose(PAIRS - 1, 1, False)


def kernel(**inputs):
    import numpy as np
    import concourse.bacc as bacc
    from concourse.bass_utils import run_bass_kernel_spmd

    def lay(name, prefix="L0_"):
        return np.asarray(inputs[prefix + name])

    x = np.asarray(inputs["x"])
    B, C, Hh, Ww = x.shape
    S = 16
    gh, gw = Hh // S, Ww // S
    KT = C * S * S // P
    patches = x.reshape(B, C, gh, S, gw, S).transpose(0, 1, 3, 5, 2, 4).reshape(B, KT, P, gh * gw)
    w = lay("tok_W")
    arrays = {
        "x": patches.transpose(0, 2, 1, 3),
        "cls": np.asarray(inputs["cls_tok"]).reshape(1, D),
        "w_tok": w.T.reshape(KT, P, D).transpose(1, 0, 2),
        "tok_b": lay("tok_b"),
        "wdq": lay("attn_W_DQ"), "wuqT": lay("attn_W_UQ").T,
        "wdkv": lay("attn_W_DKV").reshape(2, P, HD).transpose(1, 0, 2),
        "wukvT": lay("attn_W_UKV").T.reshape(2, P, 2 * HD).transpose(1, 0, 2),
        "wqr": lay("attn_W_QR"), "wkr": lay("attn_W_KR"), "woT": lay("attn_W_O").T,
        "wq": lay("attn_q_norm_w"), "wk": lay("attn_k_norm_w"), "ar": lay("ffn_adaptive_range"),
    }
    for n in ("cn_w1", "cn_b1", "cn_w2", "cn_b2", "cn_w3", "cn_b3", "cn_w4", "cn_b4",
              "gc_w1", "gc_b1", "gc_w2", "gc_b2", "gc_w3", "gc_b3"):
        arrays[n] = lay("ffn_" + n)
    arrays["cn_b1"] = arrays["cn_b1"].reshape(-1, P).T

    nc = bacc.Bacc("TRN2", target_bir_lowering=False, num_devices=1)
    feeds, aps = {}, {}
    for n, arr in arrays.items():
        arr = np.ascontiguousarray(arr)
        feeds[f"in_{n}"] = arr
        aps[n] = nc.dram_tensor(f"in_{n}", arr.shape, mybir.dt.from_np(arr.dtype), kind="ExternalInput").ap()
    shape = (B, gh * gw + 1, D)
    out = nc.dram_tensor("out", shape, F32, kind="ExternalOutput").ap()
    build(nc, aps, out)
    r = run_bass_kernel_spmd(nc, [feeds], core_ids=[0])
    return r.results[0]["out"]
```
